# Optimizing a Trainium2 kernel written in Bass

```python
import numpy as np
import jax
import jax.numpy as jnp

def _softmax(x, axis=-1):
    return jax.nn.softmax(x, axis=axis)

def _gelu(x):
    return jax.nn.gelu(x, approximate=True)

def _silu(x):
    return jax.nn.silu(x)

def _sigmoid(x):
    return jax.nn.sigmoid(x)

def _layernorm(x, axis=-1, eps=1e-05):
    m = jnp.mean(x, axis=axis, keepdims=True)
    v = jnp.var(x, axis=axis, keepdims=True)
    return (x - m) / jnp.sqrt(v + eps)

def _scatter_add(tgt, idx, src, axis=0):
    return tgt.at[idx].add(src)

def _segment_sum(src, seg, n):
    return jax.ops.segment_sum(src, seg, n)
kernel_name = 'mk_early_fusion_d1_tok_img512_r4_22b54b'

def setup_inputs(seed: int=0):
    np.random.seed(seed)
    _w = jnp.asarray

    def _rec_inputs():
        import jax
        import jax.numpy as jnp
        _rk = jax.random.key(seed)
        x = -0.000356955 + 1 * jax.random.normal(jax.random.fold_in(_rk, 1), (8, 3, 112, 112), jnp.float32)
        txt = -0.000284838 + 0.576988 * jax.random.normal(jax.random.fold_in(_rk, 2), (8, 128, 128), jnp.float32)
        return (x, txt)
    x, txt = _rec_inputs()

    def _L0_tok_setup():
        import jax, jax.numpy as jnp
        import numpy as np
        IMG = 112
        P = 16
        C = 3
        D = 128
        DC = 8
        DS = 4
        NH = IMG // P
        NPATCH = NH * NH
        PDIM = C * P * P
        BATCH = 32
        EPS = 1e-05
        key = jax.random.key(seed)
        ks = jax.random.split(key, 10)

        def lin(k, fan_in, shape):
            bound = 1.0 / np.sqrt(fan_in)
            return jax.random.uniform(k, shape, jnp.float32, -bound, bound)
        return {'images': jax.random.normal(ks[0], (BATCH, C, IMG, IMG), jnp.float32), 'W_patch': lin(ks[1], PDIM, (PDIM, D)), 'b_patch': jnp.zeros((D,), jnp.float32), 'pos_embed': jax.random.normal(ks[2], (1, NPATCH, D), jnp.float32) * 0.02, 'W_coord': lin(ks[3], D, (D, DC)), 'b_coord': jnp.zeros((DC,), jnp.float32), 'W_spinor': lin(ks[4], D, (D, DS)), 'b_spinor': jnp.zeros((DS,), jnp.float32), 'W_embed': lin(ks[5], DC, (DC, D)), 'b_embed': jnp.zeros((D,), jnp.float32), 'ln_gamma': jnp.ones((D,), jnp.float32), 'ln_beta': jnp.zeros((D,), jnp.float32), 'W_out': lin(ks[6], D, (D, D)), 'b_out': jnp.zeros((D,), jnp.float32)}
    _L0_tok_all = _L0_tok_setup()
    _L0_tok_in = {k: v for k, v in _L0_tok_all.items() if k in ('W_patch', 'b_patch', 'pos_embed', 'W_coord', 'b_coord', 'W_spinor', 'b_spinor', 'W_embed', 'b_embed', 'ln_gamma', 'ln_beta', 'W_out', 'b_out')}
    del _L0_tok_all

    def _L0_attn_setup():
        import jax, jax.numpy as jnp
        import numpy as np
        import math
        D_MODEL = 128
        NUM_HEADS = 8
        LN_EPS = 1e-05
        key = jax.random.key(seed)
        ks = jax.random.split(key, 8)
        B, L, D = (2, 512, D_MODEL)
        x = jax.random.normal(ks[0], (B, L, D), dtype=jnp.float32)
        s = 0.02
        return {'x': x, 'W_qkv': jax.random.normal(ks[1], (D, 3 * D), dtype=jnp.float32) * s, 'b_qkv': jnp.zeros((3 * D,), dtype=jnp.float32), 'W_out': jax.random.normal(ks[2], (D, D), dtype=jnp.float32) * s, 'b_out': jnp.zeros((D,), dtype=jnp.float32), 'decay_logits': jnp.zeros((NUM_HEADS,), dtype=jnp.float32), 'ln_g': jnp.ones((D,), dtype=jnp.float32), 'ln_b': jnp.zeros((D,), dtype=jnp.float32)}
    _L0_attn_all = _L0_attn_setup()
    _L0_attn_in = {k: v for k, v in _L0_attn_all.items() if k in ('W_qkv', 'b_qkv', 'W_out', 'b_out', 'decay_logits', 'ln_g', 'ln_b')}
    del _L0_attn_all

    def _L0_ffn_setup():
        import jax, jax.numpy as jnp
        import numpy as np
        B, S, D = (32, 128, 128)
        E, H, O, K = (8, 512, 128, 2)
        key = jax.random.key(seed)
        ks = jax.random.split(key, 5)
        sc = lambda k, shape, scale: jax.random.normal(k, shape, jnp.float32) * scale
        return {'x': sc(ks[0], (B, S, D), 1.0), 'attn_w': sc(ks[1], (D, 1), 0.05), 'attn_b': jnp.zeros((1,), jnp.float32), 'gate_w': sc(ks[2], (D, E), 0.05), 'gate_b': jnp.zeros((E,), jnp.float32), 'w1': sc(ks[3], (E, D, H), 0.02), 'b1': jnp.zeros((E, H), jnp.float32), 'w2': sc(ks[4], (E, H, O), 0.02), 'b2': jnp.zeros((E, O), jnp.float32)}
    _L0_ffn_all = _L0_ffn_setup()
    _L0_ffn_in = {k: v for k, v in _L0_ffn_all.items() if k in ('attn_w', 'attn_b', 'gate_w', 'gate_b', 'w1', 'b1', 'w2', 'b2')}
    del _L0_ffn_all
    return {'x': x, 'txt': txt, 'L0_tok_W_patch': _L0_tok_in['W_patch'], 'L0_tok_b_patch': _L0_tok_in['b_patch'], 'L0_tok_pos_embed': _L0_tok_in['pos_embed'], 'L0_tok_W_coord': _L0_tok_in['W_coord'], 'L0_tok_b_coord': _L0_tok_in['b_coord'], 'L0_tok_W_spinor': _L0_tok_in['W_spinor'], 'L0_tok_b_spinor': _L0_tok_in['b_spinor'], 'L0_tok_W_embed': _L0_tok_in['W_embed'], 'L0_tok_b_embed': _L0_tok_in['b_embed'], 'L0_tok_ln_gamma': _L0_tok_in['ln_gamma'], 'L0_tok_ln_beta': _L0_tok_in['ln_beta'], 'L0_tok_W_out': _L0_tok_in['W_out'], 'L0_tok_b_out': _L0_tok_in['b_out'], 'L0_attn_W_qkv': _L0_attn_in['W_qkv'], 'L0_attn_b_qkv': _L0_attn_in['b_qkv'], 'L0_attn_W_out': _L0_attn_in['W_out'], 'L0_attn_b_out': _L0_attn_in['b_out'], 'L0_attn_decay_logits': _L0_attn_in['decay_logits'], 'L0_attn_ln_g': _L0_attn_in['ln_g'], 'L0_attn_ln_b': _L0_attn_in['ln_b'], 'L0_ffn_attn_w': _L0_ffn_in['attn_w'], 'L0_ffn_attn_b': _L0_ffn_in['attn_b'], 'L0_ffn_gate_w': _L0_ffn_in['gate_w'], 'L0_ffn_gate_b': _L0_ffn_in['gate_b'], 'L0_ffn_w1': _L0_ffn_in['w1'], 'L0_ffn_b1': _L0_ffn_in['b1'], 'L0_ffn_w2': _L0_ffn_in['w2'], 'L0_ffn_b2': _L0_ffn_in['b2']}

def reference(x, txt, L0_tok_W_patch, L0_tok_b_patch, L0_tok_pos_embed, L0_tok_W_coord, L0_tok_b_coord, L0_tok_W_spinor, L0_tok_b_spinor, L0_tok_W_embed, L0_tok_b_embed, L0_tok_ln_gamma, L0_tok_ln_beta, L0_tok_W_out, L0_tok_b_out, L0_attn_W_qkv, L0_attn_b_qkv, L0_attn_W_out, L0_attn_b_out, L0_attn_decay_logits, L0_attn_ln_g, L0_attn_ln_b, L0_ffn_attn_w, L0_ffn_attn_b, L0_ffn_gate_w, L0_ffn_gate_b, L0_ffn_w1, L0_ffn_b1, L0_ffn_w2, L0_ffn_b2):
    import jax
    import jax.numpy as jnp

    def _L0_tok_ref(images, W_patch, b_patch, pos_embed, W_coord, b_coord, W_spinor, b_spinor, W_embed, b_embed, ln_gamma, ln_beta, W_out, b_out):
        import jax, jax.numpy as jnp
        import numpy as np
        IMG = 112
        P = 16
        C = 3
        D = 128
        DC = 8
        DS = 4
        NH = IMG // P
        NPATCH = NH * NH
        PDIM = C * P * P
        BATCH = 32
        EPS = 1e-05
        B = images.shape[0]
        patches = images.reshape(B, C, NH, P, NH, P)
        patches = patches.transpose(0, 2, 4, 1, 3, 5).reshape(B, NPATCH, PDIM)
        x = patches @ W_patch + b_patch + pos_embed
        coords = x @ W_coord + b_coord
        spinor = x @ W_spinor + b_spinor
        K0 = jnp.sum(spinor * spinor, axis=-1)
        x_manifold = coords @ W_embed + b_embed
        x_enh = x_manifold * K0[..., None] + x
        mu = jnp.mean(x_enh, axis=-1, keepdims=True)
        var = jnp.mean(jnp.square(x_enh - mu), axis=-1, keepdims=True)
        x_norm = (x_enh - mu) * jax.lax.rsqrt(var + EPS) * ln_gamma + ln_beta
        return x_norm @ W_out + b_out

    def _L0_attn_ref(x, W_qkv, b_qkv, W_out, b_out, decay_logits, ln_g, ln_b):
        import jax, jax.numpy as jnp
        import numpy as np
        import math
        D_MODEL = 128
        NUM_HEADS = 8
        LN_EPS = 1e-05
        B, L, D = x.shape
        H = NUM_HEADS
        E = D // H
        qkv = x @ W_qkv + b_qkv
        q, k, v = jnp.split(qkv, 3, axis=-1)
        q = q.reshape(B, L, H, E)
        k = k.reshape(B, L, H, E)
        v = v.reshape(B, L, H, E)
        q = (jax.nn.elu(q) + 1.0) / math.sqrt(E)
        k = jax.nn.elu(k) + 1.0
        lam = 0.99 + 0.01 * jax.nn.sigmoid(decay_logits)
        lam = lam.reshape(1, 1, H, 1)
        idx = jnp.arange(L, dtype=jnp.float32).reshape(1, L, 1, 1)
        decay_k = lam ** (-idx)
        decay_q = lam ** idx
        k_d = k * decay_k
        kv = jnp.einsum('blhe,blhf->blhef', k_d, v)
        mem = jnp.cumsum(kv, axis=1)
        k_sum = jnp.cumsum(k_d, axis=1)
        q_d = q * decay_q
        num = jnp.einsum('blhe,blhef->blhf', q_d, mem)
        den = jnp.einsum('blhe,blhe->blh', q_d, k_sum)[..., None] + 1e-06
        out = (num / den).reshape(B, L, D)
        out = out @ W_out + b_out
        mu = jnp.mean(out, axis=-1, keepdims=True)
        var = jnp.var(out, axis=-1, keepdims=True)
        return (out - mu) / jnp.sqrt(var + LN_EPS) * ln_g + ln_b

    def _L0_ffn_ref(x, attn_w, attn_b, gate_w, gate_b, w1, b1, w2, b2):
        import jax, jax.numpy as jnp
        import numpy as np
        B, S, D = (32, 128, 128)
        E, H, O, K = (8, 512, 128, 2)
        scores = x @ attn_w + attn_b
        aw = jax.nn.softmax(scores, axis=1)
        pooled = jnp.sum(x * aw, axis=1)
        gates = jax.nn.softmax(pooled @ gate_w + gate_b, axis=-1)
        _, idx = jax.lax.top_k(gates, K)
        mask = jnp.sum(jax.nn.one_hot(idx, E, dtype=gates.dtype), axis=-2)
        g = gates * mask
        g = g / (jnp.sum(g, axis=-1, keepdims=True) + 1e-09)
        h = jax.nn.gelu(jnp.einsum('bsd,edh->ebsh', x, w1) + b1[:, None, None, :], approximate=False)
        eo = jax.nn.gelu(jnp.einsum('ebsh,eho->ebso', h, w2) + b2[:, None, None, :], approximate=False)
        return jnp.einsum('ebso,be->bso', eo, g)
    h = _L0_tok_ref(x, L0_tok_W_patch, L0_tok_b_patch, L0_tok_pos_embed, L0_tok_W_coord, L0_tok_b_coord, L0_tok_W_spinor, L0_tok_b_spinor, L0_tok_W_embed, L0_tok_b_embed, L0_tok_ln_gamma, L0_tok_ln_beta, L0_tok_W_out, L0_tok_b_out)
    h = jnp.concatenate([h, txt], axis=1)
    h = h + _L0_attn_ref(_layernorm(h, axis=-1), L0_attn_W_qkv, L0_attn_b_qkv, L0_attn_W_out, L0_attn_b_out, L0_attn_decay_logits, L0_attn_ln_g, L0_attn_ln_b)
    h = h + _L0_ffn_ref(_layernorm(h, axis=-1), L0_ffn_attn_w, L0_ffn_attn_b, L0_ffn_gate_w, L0_ffn_gate_b, L0_ffn_w1, L0_ffn_b1, L0_ffn_w2, L0_ffn_b2)
    return h

_drawn_inputs = setup_inputs


def setup_inputs(seed=0):
    import zlib

    import numpy as np

    out = dict(_drawn_inputs(seed))
    spreads = {'L0_tok_b_patch': (0.0, 0.1),
     'L0_tok_b_coord': (0.0, 0.281),
     'L0_tok_b_spinor': (0.0, 0.347),
     'L0_tok_b_embed': (0.0, 0.1),
     'L0_tok_ln_gamma': (1.0, 0.2),
     'L0_tok_ln_beta': (0.0, 0.1),
     'L0_tok_b_out': (0.0, 0.1),
     'L0_attn_b_qkv': (0.0, 0.1),
     'L0_attn_b_out': (0.0, 0.1),
     'L0_attn_decay_logits': (0.0, 0.8),
     'L0_attn_ln_g': (1.0, 0.2),
     'L0_attn_ln_b': (0.0, 0.1),
     'L0_ffn_gate_b': (0.0, 0.8),
     'L0_ffn_b1': (0.0, 0.8),
     'L0_ffn_b2': (0.0, 0.1)}
    factors = {'L0_tok_pos_embed': 5.663, 'L0_ffn_attn_w': 6.902, 'L0_ffn_w1': 3.426, 'L0_ffn_w2': 3.215}
    for name, (base, spread) in spreads.items():
        noise = np.random.default_rng([zlib.crc32(name.encode()), seed]).standard_normal(out[name].shape)
        drawn = base * np.exp(spread * noise) if base else spread * noise
        out[name] = jnp.asarray(drawn.astype(out[name].dtype))
    for name, factor in factors.items():
        out[name] = (out[name] * factor).astype(out[name].dtype)
    return out
```

```python
from contextlib import ExitStack

import numpy as np

import concourse.bass as bass
from concourse import mybir

F32 = mybir.dt.float32
I32 = mybir.dt.int32
U32 = mybir.dt.uint32
ALU = mybir.AluOpType
ACT = mybir.ActivationFunctionType
AX_X = mybir.AxisListType.X

BATCH, CHANNELS, IMAGE, PATCH = 8, 3, 112, 16
GRID = IMAGE // PATCH
PATCHES = GRID * GRID
PATCH_DIM = CHANNELS * PATCH * PATCH
PATCH_CHUNKS = PATCH_DIM // 128
TEXT = 128
D = 128
COORDS, SPINOR = 8, 4
SPINOR_AT = 32
SEQ = PATCHES + TEXT
COLS = BATCH * SEQ
TOK_COLS = BATCH * PATCHES
HEADS = 8
HEAD = D // HEADS
EXPERTS, HIDDEN, TOP = 8, 512, 2
HID_CHUNKS = HIDDEN // 128
EPS = 1e-5

PER = 2
GROUPS = BATCH // PER
GC = PER * SEQ
BANK = 512
LO = 128
HI = SEQ - LO
UNITS = BATCH * TOP

MATS = [("coord_spinor", D), ("embed", D), ("tok_out", D), ("qkv", 3 * D), ("attn_out", D), ("gate", EXPERTS),
        ("bias_v", D), ("bias_gate", EXPERTS), ("pos", PATCHES),
        ("ones_mean", D), ("spinor_sum", D), ("block_ones", D), ("causal", LO), ("position", SEQ),
        ("diag", BATCH * TOP)]
VECS = ["b_patch", "b_coord_spinor", "b_embed", "tok_gamma", "tok_beta", "b_tok_out", "b_q", "b_k", "b_attn_out",
        "decay", "attn_gamma", "attn_beta", "pool_w", "pool_b"]
AT = {}
for _name, _n in MATS + [(_v, 1) for _v in VECS]:
    AT[_name] = (sum(n for _, n in AT.values()), _n)
PARAM_COLS = sum(n for _, n in AT.values())
W1_AT, W2_AT, B1_AT, B2_AT = 0, HIDDEN, 2 * HIDDEN, 2 * HIDDEN + HID_CHUNKS
EXPERT_COLS = B2_AT + 1


class NormSemaphores:

    def __init__(self, sem, name):
        self.mean_done = sem(f"{name}_mean_done")
        self.centered = sem(f"{name}_centered")
        self.squared = sem(f"{name}_squared")
        self.var_done = sem(f"{name}_var_done")
        self.log = sem(f"{name}_log")
        self.rstd_ready = sem(f"{name}_rstd_ready")
        self.normed = sem(f"{name}_normed")


def build(nc, patches, text, w_patch, params, experts, out):
    ctx = ExitStack()
    with ctx:
        def sb(name, shape, dt=F32):
            return ctx.enter_context(nc.sbuf_tensor(name, shape, dt))

        def sem(name):
            return ctx.enter_context(nc.semaphore(name))

        prm = sb("prm", [128, PARAM_COLS])
        patch_in = sb("patch_in", [128, PATCH_CHUNKS, TOK_COLS])
        patch_w = sb("patch_w", [128, PATCH_CHUNKS, D])
        expert_w = sb("expert_w", [128, EXPERTS, EXPERT_COLS])
        x_tok = sb("x_tok", [128, TOK_COLS])
        coord_spin = sb("coord_spin", [128, TOK_COLS])
        manifold = patch_in[:, 0, :]
        x_enh = patch_in[:, 1, :]
        tok_c = patch_in[:, 2, :]
        tok_sq = patch_in[:, 3, :]
        tok_rstd = patch_in[:, 4, :]
        tok_n = patch_in[:, 5, :]
        h = sb("h", [128, COLS])
        h_beta = sb("h_beta", [128, COLS])

        centered = sb("centered", [128, COLS])
        squares = sb("squares", [128, COLS])
        rstd = sb("rstd", [128, COLS])
        xn = sb("xn", [128, COLS])
        q_exp = sb("q_exp", [128, COLS])
        q_pos = sb("q_pos", [128, COLS])
        q_elu = sb("q_elu", [128, COLS])
        k_exp = sb("k_exp", [128, COLS])
        k_pos = sb("k_pos", [128, COLS])
        k_elu = sb("k_elu", [128, COLS])
        q_dec = sb("q_dec", [128, COLS])
        k_dec = sb("k_dec", [128, COLS])
        k_sum = k_exp
        h1 = q_dec
        logvar = k_pos
        qk_sum = k_pos
        den = q_exp
        rden = q_pos
        att = q_elu
        q_heads = sb("q_heads", [128, HEADS, COLS])
        decay_q = sb("decay_q", [128, SEQ])
        decay_k = sb("decay_k", [128, SEQ])
        ones = sb("ones", [128, SEQ])
        lam = sb("lam", [128, 8])
        w_out_c = sb("w_out_c", [128, D])
        out_stat = sb("out_stat", [128, 4])
        pool_w128 = sb("pool_w128", [128, 128])
        eps_col = sb("eps_col", [128, 2])
        x_fix = [sb(f"x_fix{p}", [128, SEQ]) for p in range(2)]
        k_fix = [sb(f"k_fix{p}", [128, SEQ]) for p in range(2)]
        v_lo = [sb(f"v_lo{p}", [128, HEADS, 2 * HEAD]) for p in range(2)]
        v_hi = [sb(f"v_hi{p}", [128, HEADS, 2 * HEAD]) for p in range(2)]
        s_lo = [sb(f"s_lo{p}", [128, HEADS, SEQ]) for p in range(2)]
        s_hi = [sb(f"s_hi{p}", [HI, HEADS, HI]) for p in range(2)]
        attn_x = k_exp
        pool_exp = squares
        score_max = sb("score_max", [128, BATCH])
        score_shift = sb("score_shift", [128, BATCH])
        score_bias = sb("score_bias", [128, BATCH])
        exp_sum = sb("exp_sum", [128, BATCH])
        exp_rsum = sb("exp_rsum", [128, BATCH])
        pooled_raw = sb("pooled_raw", [128, BATCH])
        pooled = sb("pooled", [128, BATCH])
        scratch = sb("scratch", [128, SEQ])
        gl = sb("gl", [BATCH, 8, EXPERTS])
        gate_idx = sb("gate_idx", [BATCH, EXPERTS], U32)
        gate_cat = sb("gate_cat", [BATCH, 2, TOP])
        gate_rows = sb("gate_rows", [BATCH, 2, UNITS])
        gate_all = sb("gate_all", [128, UNITS])
        expert_of = sb("expert_of", [1, UNITS], I32)
        w_fix = [q_heads[:, k, 0:EXPERT_COLS] for k in range(4)]
        hid = [q_heads[:, 4 + k, 0:HID_CHUNKS * SEQ].rearrange("p (c l) -> p c l", c=HID_CHUNKS) for k in range(2)]
        eo = [sb(f"eo{k}", [128, SEQ]) for k in range(2)]
        acc = sb("acc", [128, SEQ])
        out_sb = k_elu
        ps = ctx.enter_context(nc.psum_tensor("ps", [128, 8 * BANK], F32))

        def P(name):
            at, n = AT[name]
            return prm[:, at:at + n]

        def bank(k, n=GC, rows=slice(0, 128), at=0):
            return ps[rows, k * BANK + at:k * BANK + at + n]

        def gbank(g, k=0):
            return ps[:, bass.ds(g * BANK + k * BANK, GC)]

        def gcols(t, g):
            return t[:, bass.ds(g * GC, GC)]

        def bcols(t, b):
            return t[:, bass.ds(b * SEQ, SEQ)]

        patches_loaded = sem("patches_loaded")
        params_loaded = sem("params_loaded")
        text_loaded = sem("text_loaded")
        experts_loaded = sem("experts_loaded")
        embed_done = sem("embed_done")
        x_ready = sem("x_ready")
        coords_done = sem("coords_done")
        coord_spin_ready = sem("coord_spin_ready")
        manifold_done = sem("manifold_done")
        manifold_ready = sem("manifold_ready")
        enh_mul = sem("enh_mul")
        enh_ready = sem("enh_ready")
        tok_mean_done = sem("tok_mean_done")
        tok_centered = sem("tok_centered")
        tok_squared = sem("tok_squared")
        tok_var_done = sem("tok_var_done")
        tok_log = sem("tok_log")
        tok_rstd_ready = sem("tok_rstd_ready")
        tok_mul = sem("tok_mul")
        tok_normed = sem("tok_normed")
        tok_out_done = sem("tok_out_done")
        tok_in_h = sem("tok_in_h")
        h_beta_ready = sem("h_beta_ready")
        out_done = sem("out_done")
        out_mul = sem("out_mul")
        h1_ready = sem("h1_ready")
        setup_vec = sem("setup_vec")
        setup_act = sem("setup_act")
        setup_pool = sem("setup_pool")
        w_out_c_ready = sem("w_out_c_ready")
        bias_mean_done = sem("bias_mean_done")
        decay_ready = sem("decay_ready")
        q_done = sem("q_done")
        k_done = sem("k_done")
        q_exp_ready = sem("q_exp_ready")
        k_exp_ready = sem("k_exp_ready")
        k_pos_ready = sem("k_pos_ready")
        q_elu_ready = sem("q_elu_ready")
        k_elu_ready = sem("k_elu_ready")
        q_dec_ready = sem("q_dec_ready")
        k_dec_ready = sem("k_dec_ready")
        q_heads_loaded = sem("q_heads_loaded")
        k_sum_ready = sem("k_sum_ready")
        qk_sum_ready = sem("qk_sum_ready")
        den_done = sem("den_done")
        den_ready = sem("den_ready")
        rden_ready = sem("rden_ready")
        fix_ready = sem("fix_ready")
        v_done = sem("v_done")
        v_ready = sem("v_ready")
        lo_done = sem("lo_done")
        lo_masked = sem("lo_masked")
        lo_copied = sem("lo_copied")
        hi_done = sem("hi_done")
        hi_masked = sem("hi_masked")
        av_done = sem("av_done")
        att_ready = sem("att_ready")
        score_done = sem("score_done")
        score_max_ready = sem("score_max_ready")
        score_shift_ready = sem("score_shift_ready")
        score_bias_ready = sem("score_bias_ready")
        pool_exp_ready = sem("pool_exp_ready")
        pooled_step = sem("pooled_step")
        pooled_ready = sem("pooled_ready")
        gate_done = sem("gate_done")
        gate_step = sem("gate_step")
        gate_exp_ready = sem("gate_exp_ready")
        gate_rows_ready = sem("gate_rows_ready")
        gate_bcast_done = sem("gate_bcast_done")
        gates_ready = sem("gates_ready")
        w_fixed = sem("w_fixed")
        up_done = sem("up_done")
        hid_ready = sem("hid_ready")
        down_done = sem("down_done")
        eo_ready = sem("eo_ready")
        acc_ready = sem("acc_ready")
        out_stored = sem("out_stored")

        ln1, ln2, ln3 = NormSemaphores(sem, "ln1"), NormSemaphores(sem, "ln2"), NormSemaphores(sem, "ln3")

        block = ctx.enter_context(nc.Block())

        @block.sync
        def _(sp):
            sp.dma_start(patch_w[:], w_patch).then_inc(patches_loaded, 16)
            sp.dma_start(patch_in[:], patches).then_inc(patches_loaded, 16)
            h_text = h[:, :].rearrange("p (b l) -> p b l", b=BATCH)[:, :, PATCHES:SEQ]
            sp.dma_start(h_text, text).then_inc(text_loaded, 16)
            sp.dma_start(expert_w[:], experts).then_inc(experts_loaded, 16)
            sp.wait_ge(setup_pool, 1)
            with sp.Fori(0, GROUPS) as g:
                at = sp.snap(g * GC)
                sp.wait_ge(q_dec_ready, g + 1)
                for hd in range(HEADS):
                    rows = slice(HEAD * hd, HEAD * hd + HEAD)
                    sp.dma_start(q_heads[rows, hd, bass.ds(at, GC)],
                                 q_dec[rows, bass.ds(at, GC)]).then_inc(q_heads_loaded, 16)
            with sp.Fori(0, BATCH) as b:
                at = sp.snap(b * SEQ)
                added = sp.snap(b * TOP + TOP)
                sp.wait_ge(acc_ready, added)
                sp.dma_start(out[:, bass.ds(at, SEQ)], out_sb[:, bass.ds(at, SEQ)]).then_inc(out_stored, 16)
            sp.wait_ge(out_stored, 16 * BATCH)

        @block.gpsimd
        def _(pool):
            nc.gpsimd.memset(q_heads[:], 0.0).then_inc(setup_pool, 1)
            pool.wait_ge(text_loaded, 16)
            pool.wait_ge(tok_in_h, 1)
            pool.wait_ge(params_loaded, 16)
            nc.gpsimd.tensor_scalar(h_beta[:], h[:], P("attn_beta"), None, ALU.add).then_inc(h_beta_ready, 1)
            pool.wait_ge(decay_ready, 3)
            with pool.Fori(0, GROUPS) as g:
                for src, dec, dst, got, made in ((q_elu, decay_q, q_dec, q_elu_ready, q_dec_ready),
                                                 (k_elu, decay_k, k_dec, k_elu_ready, k_dec_ready)):
                    pool.wait_ge(got, g + 1)
                    nc.gpsimd.tensor_tensor(gcols(dst, g).rearrange("p (b l) -> p b l", b=PER),
                                            gcols(src, g).rearrange("p (b l) -> p b l", b=PER),
                                            dec[:, :].unsqueeze(1).to_broadcast([128, PER, SEQ]),
                                            ALU.mult).then_inc(made, 1)
            with pool.Fori(0, GROUPS) as g:
                pool.wait_ge(k_sum_ready, (g + 1) * PER)
                nc.gpsimd.tensor_tensor(gcols(qk_sum, g), gcols(q_dec, g), gcols(k_sum, g),
                                        ALU.mult).then_inc(qk_sum_ready, 1)

            def fix(b, p):
                nc.gpsimd.tensor_copy(x_fix[p][:], bcols(xn, b)).then_inc(fix_ready, 1)
                nc.gpsimd.tensor_copy(k_fix[p][:], bcols(k_dec, b)).then_inc(fix_ready, 1)

            pool.wait_ge(ln1.normed, GROUPS)
            pool.wait_ge(k_dec_ready, GROUPS)
            fix(0, 0)
            fix(1, 1)
            with pool.Fori(1, GROUPS) as i:
                for p in range(2):
                    pool.wait_ge(hi_done, i * 2 + (p - 1))
                    fix(i * 2 + p, p)

            def fetch(u, k):
                e = pool.value_load(expert_of[0:1, bass.ds(u, 1)], min_val=0, max_val=EXPERTS - 1)
                nc.gpsimd.tensor_copy(
                    w_fix[k], expert_w[:, bass.ds(e, 1), :].rearrange("p a n -> p (a n)")
                ).then_inc(w_fixed, 1)

            pool.wait_ge(experts_loaded, 16)
            pool.wait_ge(gates_ready, 2)
            for k in range(4):
                fetch(k, k)
            with pool.Fori(1, UNITS // 4) as i:
                for k in range(4):
                    pool.wait_ge(eo_ready, i * 4 + (k - 3))
                    fetch(i * 4 + k, k)

        @block.scalar
        def _(act):
            nc.scalar.dma_start(prm[:], params).then_inc(params_loaded, 16)
            nc.scalar.preload_act_table_set("natural_log_exp_and_others")
            act.wait_ge(params_loaded, 16)
            nc.scalar.activation(lam[:, 0:1], P("decay"), ACT.Exp, scale=-1.0).then_inc(setup_act, 1)
            act.wait_ge(setup_vec, 7)
            nc.scalar.activation(lam[:, 4:5], lam[:, 3:4], ACT.Ln).then_inc(setup_act, 1)
            act.wait_ge(setup_act, 2)
            nc.scalar.mul(lam[:, 5:6], lam[:, 4:5], -1.0).then_inc(setup_act, 1)
            act.wait_ge(setup_act, 3)
            nc.scalar.activation(decay_q[:], P("position"), ACT.Exp, scale=lam[:, 4:5]).then_inc(decay_ready, 1)
            nc.scalar.activation(decay_k[:], P("position"), ACT.Exp, scale=lam[:, 5:6]).then_inc(decay_ready, 1)

            act.wait_ge(coords_done, 1)
            nc.scalar.activation(coord_spin[0:COORDS, :], bank(1, TOK_COLS, slice(0, COORDS)), ACT.Identity,
                                 bias=P("b_coord_spinor")[0:COORDS, :]).then_inc(coord_spin_ready, 1)
            sp_rows = slice(SPINOR_AT, SPINOR_AT + SPINOR)
            nc.scalar.activation(coord_spin[sp_rows, :], bank(1, TOK_COLS, sp_rows), ACT.Square,
                                 bias=P("b_coord_spinor")[sp_rows, :]).then_inc(coord_spin_ready, 1)
            act.wait_ge(manifold_done, 1)
            nc.scalar.activation(manifold, bank(2, TOK_COLS), ACT.Identity,
                                 bias=P("b_embed")).then_inc(manifold_ready, 1)
            act.wait_ge(tok_centered, 1)
            nc.scalar.activation(tok_sq, tok_c, ACT.Square).then_inc(tok_squared, 1)
            act.wait_ge(tok_var_done, 1)
            nc.scalar.activation(tok_sq, bank(5, TOK_COLS), ACT.Ln, bias=eps_col[:, 0:1]).then_inc(tok_log, 1)
            act.wait_ge(tok_log, 1)
            nc.scalar.activation(tok_rstd, tok_sq, ACT.Exp, scale=-0.5).then_inc(tok_rstd_ready, 1)

            def squares_of(ln):
                with act.Fori(0, GROUPS) as g:
                    act.wait_ge(ln.centered, g + 1)
                    nc.scalar.activation(gcols(squares, g), gcols(centered, g),
                                         ACT.Square).then_inc(ln.squared, 1)

            def rstd_of(ln):
                with act.Fori(0, GROUPS) as g:
                    act.wait_ge(ln.var_done, g + 1)
                    nc.scalar.activation(gcols(logvar, g), gbank(g, 4), ACT.Ln,
                                         bias=eps_col[:, 0:1]).then_inc(ln.log, 1)
                    act.wait_ge(ln.log, g + 1)
                    nc.scalar.activation(gcols(rstd, g), gcols(logvar, g), ACT.Exp,
                                         scale=-0.5).then_inc(ln.rstd_ready, 1)

            squares_of(ln1)
            rstd_of(ln1)
            with act.Fori(0, GROUPS) as g:
                act.wait_ge(q_done, g + 1)
                nc.scalar.activation(gcols(q_exp, g), gbank(g), ACT.Exp, bias=P("b_q")).then_inc(q_exp_ready, 1)
                nc.scalar.activation(gcols(q_pos, g), gbank(g), ACT.Relu, bias=P("b_q")).then_inc(q_exp_ready, 1)
                act.wait_ge(k_done, g + 1)
                nc.scalar.activation(gcols(k_exp, g), gbank(g, 4), ACT.Exp,
                                     bias=P("b_k")).then_inc(k_exp_ready, 1)
            with act.Fori(0, GROUPS) as g:
                act.wait_ge(den_done, g + 1)
                nc.scalar.activation(gcols(den, g), gbank(g), ACT.Identity,
                                     bias=eps_col[:, 1:2]).then_inc(den_ready, 1)

            def copy_lo(b, p):
                for pair in range(HEADS // 2):
                    act.wait_ge(lo_masked, b * 4 + (pair + 1))
                    nc.scalar.activation(
                        s_lo[p][:, 2 * pair:2 * pair + 2, LO:SEQ],
                        bank(pair).rearrange("p (a l) -> p a l", a=2)[:, :, LO:SEQ],
                        ACT.Copy).then_inc(lo_copied, 1)

            copy_lo(0, 0)
            copy_lo(1, 1)
            with act.Fori(1, GROUPS) as i:
                for p in range(2):
                    act.wait_ge(av_done, i * 2 + (p - 1))
                    copy_lo(i * 2 + p, p)

            with act.Fori(0, GROUPS) as g:
                act.wait_ge(out_done, g + 1)
                nc.scalar.activation(gcols(squares, g), gbank(g), ACT.Square,
                                     bias=out_stat[:, 3:4]).then_inc(ln2.centered, 1)
                nc.scalar.activation(gcols(centered, g), gbank(g), ACT.Identity,
                                     bias=out_stat[:, 3:4]).then_inc(ln2.centered, 1)
            rstd_of(ln2)
            squares_of(ln3)
            rstd_of(ln3)
            act.wait_ge(score_bias_ready, 1)
            with act.Fori(0, BATCH) as b:
                nc.scalar.activation(
                    bcols(pool_exp, b),
                    ps[:, bass.ds((b // PER) * BANK + (b % PER) * SEQ, SEQ)],
                    ACT.Exp, bias=score_bias[:, bass.ds(b, 1)],
                    accum_out=exp_sum[:, bass.ds(b, 1)]).then_inc(pool_exp_ready, 1)
            act.wait_ge(gate_step, 2)
            nc.scalar.activation(gl[:, 2, :], gl[:, 0, :], ACT.Exp, bias=gl[:, 1, 0:1],
                                 accum_out=gl[:, 1, 1:2]).then_inc(gate_exp_ready, 1)
            nc.scalar.preload_act_table(ACT.Gelu)

            def gelu_hidden(u, k):
                if not isinstance(u, int) or u >= 2:
                    act.wait_ge(down_done, u - 1)
                for c in range(HID_CHUNKS):
                    if c % 2 == 0:
                        act.wait_ge(up_done, u * 2 + (c // 2 + 1))
                    ins = nc.scalar.activation(hid[k % 2][:, c, :], bank(2 * (k % 2) + c // 2, SEQ, at=(c % 2) * SEQ),
                                               ACT.Gelu, bias=w_fix[k][:, B1_AT + c:B1_AT + c + 1])
                    ins.then_inc(hid_ready, 1)

            def gelu_out(u, k):
                act.wait_ge(down_done, u + 1)
                if not isinstance(u, int) or u >= 2:
                    act.wait_ge(acc_ready, u - 1)
                nc.scalar.activation(eo[k % 2][:], bank(4 + k % 2, SEQ), ACT.Gelu,
                                     bias=w_fix[k][:, B2_AT:B2_AT + 1]).then_inc(eo_ready, 1)

            gelu_hidden(0, 0)
            for k in range(3):
                gelu_hidden(k + 1, k + 1)
                gelu_out(k, k)
            with act.Fori(1, UNITS // 4) as i:
                for k in range(4):
                    gelu_hidden(i * 4 + k, k)
                    gelu_out(i * 4 + (k - 1), (k + 3) % 4)
            gelu_out(UNITS - 1, 3)

        @block.vector
        def _(dve):
            dve.memset(eps_col[:, 0:1], EPS).then_inc(setup_vec, 1)
            dve.memset(eps_col[:, 1:2], 1e-6).then_inc(setup_vec, 1)
            dve.memset(ones[:], 1.0).then_inc(setup_vec, 1)
            dve.memset(coord_spin[:], 0.0).then_inc(setup_vec, 1)
            dve.wait_ge(setup_act, 1)
            dve.tensor_scalar(lam[:, 1:2], lam[:, 0:1], 1.0, None, ALU.add).then_inc(setup_vec, 1)
            dve.wait_ge(setup_vec, 5)
            dve.reciprocal(lam[:, 2:3], lam[:, 1:2]).then_inc(setup_vec, 1)
            dve.wait_ge(setup_vec, 6)
            dve.tensor_scalar(lam[:, 3:4], lam[:, 2:3], 0.01, 0.99, ALU.mult, ALU.add).then_inc(setup_vec, 1)
            dve.wait_ge(embed_done, 1)
            dve.scalar_tensor_tensor(
                out=x_tok[:, :].rearrange("p (b n) -> p b n", b=BATCH),
                in0=bank(0, TOK_COLS).rearrange("p (b n) -> p b n", b=BATCH), scalar=P("b_patch"),
                in1=P("pos").unsqueeze(1).to_broadcast([128, BATCH, PATCHES]),
                op0=ALU.add, op1=ALU.add).then_inc(x_ready, 1)
            for p in range(2):
                dve.memset(v_lo[p][:], 0.0).then_inc(setup_vec, 1)
                dve.memset(v_hi[p][:], 0.0).then_inc(setup_vec, 1)
            dve.wait_ge(manifold_ready, 1)
            dve.tensor_tensor(manifold, manifold, bank(3, TOK_COLS), ALU.mult).then_inc(enh_mul, 1)
            dve.wait_ge(enh_mul, 1)
            dve.tensor_tensor(x_enh, manifold, x_tok[:], ALU.add).then_inc(enh_ready, 1)
            dve.reduce_sum(out_stat[:, 0:1], P("attn_out"), axis=AX_X).then_inc(w_out_c_ready, 1)
            dve.wait_ge(w_out_c_ready, 1)
            dve.tensor_scalar(out_stat[:, 1:2], out_stat[:, 0:1], 1.0 / D, None, ALU.mult).then_inc(w_out_c_ready, 1)
            dve.wait_ge(w_out_c_ready, 2)
            dve.tensor_scalar(w_out_c[:], P("attn_out"), out_stat[:, 1:2], None,
                              ALU.subtract).then_inc(w_out_c_ready, 1)
            dve.wait_ge(tok_mean_done, 1)
            dve.tensor_tensor(tok_c, x_enh, bank(4, TOK_COLS), ALU.subtract).then_inc(tok_centered, 1)
            dve.wait_ge(decay_ready, 2)
            dve.tensor_scalar(decay_q[:], decay_q[:], float(HEAD) ** -0.5, None, ALU.mult).then_inc(decay_ready, 1)
            dve.tensor_scalar(pool_w128[:], ones[:, 0:128], P("pool_w"), None, ALU.mult).then_inc(w_out_c_ready, 1)
            dve.wait_ge(bias_mean_done, 1)
            dve.tensor_tensor(out_stat[:, 3:4], P("b_attn_out"), bank(6, 1), ALU.subtract)\
               .then_inc(w_out_c_ready, 1)
            dve.wait_ge(tok_rstd_ready, 1)
            dve.tensor_tensor(tok_n, tok_c, tok_rstd, ALU.mult).then_inc(tok_mul, 1)
            dve.wait_ge(tok_mul, 1)
            dve.tensor_scalar(tok_n, tok_n, P("tok_gamma"), P("tok_beta"), ALU.mult, ALU.add)\
               .then_inc(tok_normed, 1)
            dve.wait_ge(tok_out_done, 1)
            h_tok = h[:, :].rearrange("p (b l) -> p b l", b=BATCH)[:, :, 0:PATCHES]
            dve.tensor_scalar(h_tok, bank(7, TOK_COLS).rearrange("p (b n) -> p b n", b=BATCH),
                              P("b_tok_out"), None, ALU.add).then_inc(tok_in_h, 1)

            def center(ln, src):
                with dve.Fori(0, GROUPS) as g:
                    dve.wait_ge(ln.mean_done, g + 1)
                    dve.tensor_tensor(gcols(centered, g), gcols(src, g), gbank(g),
                                      ALU.subtract).then_inc(ln.centered, 1)

            def normalize(ln, dst):
                with dve.Fori(0, GROUPS) as g:
                    dve.wait_ge(ln.rstd_ready, g + 1)
                    dve.tensor_tensor(gcols(dst, g), gcols(centered, g), gcols(rstd, g),
                                      ALU.mult).then_inc(ln.normed, 1)

            dve.wait_ge(text_loaded, 16)
            center(ln1, h)
            normalize(ln1, xn)
            with dve.Fori(0, GROUPS) as g:
                dve.wait_ge(q_exp_ready, g * 2 + 2)
                dve.scalar_tensor_tensor(out=gcols(q_elu, g), in0=gcols(q_exp, g), scalar=1.0, in1=gcols(q_pos, g),
                                         op0=ALU.min, op1=ALU.add).then_inc(q_elu_ready, 1)
                dve.wait_ge(k_exp_ready, g + 1)
                dve.tensor_scalar(gcols(k_pos, g), gbank(g, 4), P("b_k"), 0.0, ALU.add, ALU.max)\
                   .then_inc(k_pos_ready, 1)
                dve.wait_ge(k_pos_ready, g + 1)
                dve.scalar_tensor_tensor(out=gcols(k_elu, g), in0=gcols(k_exp, g), scalar=1.0, in1=gcols(k_pos, g),
                                         op0=ALU.min, op1=ALU.add).then_inc(k_elu_ready, 1)
            dve.wait_ge(q_dec_ready, GROUPS)
            dve.wait_ge(k_dec_ready, GROUPS)
            with dve.Fori(0, BATCH) as b:
                dve.tensor_tensor_scan(bcols(k_sum, b), ones[:], bcols(k_dec, b), 0.0,
                                       ALU.mult, ALU.add).then_inc(k_sum_ready, 1)
            with dve.Fori(0, GROUPS) as g:
                dve.wait_ge(den_ready, g + 1)
                dve.reciprocal(gcols(rden, g), gcols(den, g)).then_inc(rden_ready, 1)
            dve.wait_ge(rden_ready, GROUPS)

            def masks(b, p):
                dve.wait_ge(v_done, b + 1)
                for rows, at, dst in ((128, 0, v_lo[p]), (HI, D, v_hi[p])):
                    heads = dst[0:rows, :, :].rearrange("p (j r) c -> p j (r c)", r=2)
                    for r in range(2):
                        src = bank(5, D, slice(0, rows), at).rearrange("p (j r c) -> p j r c", r=2, c=HEAD)[:, :, r, :]
                        bias = P("bias_v")[0:rows, :].rearrange("p (j r c) -> p j r c", r=2, c=HEAD)[:, :, r, :]
                        dve.tensor_tensor(heads[:, :, 3 * HEAD * r:3 * HEAD * r + HEAD], src, bias,
                                          ALU.add).then_inc(v_ready, 1)
                for pair in range(HEADS // 2):
                    dve.wait_ge(lo_done, b * 4 + (pair + 1))
                    dve.tensor_tensor(s_lo[p][:, 2 * pair:2 * pair + 2, 0:LO],
                                      bank(pair).rearrange("p (a l) -> p a l", a=2)[:, :, 0:LO],
                                      P("causal").unsqueeze(1).to_broadcast([128, 2, LO]),
                                      ALU.mult).then_inc(lo_masked, 1)
                dve.wait_ge(hi_done, b + 1)
                dve.tensor_tensor(s_hi[p][:], bank(4, HEADS * HI, slice(0, HI)).rearrange("p (a l) -> p a l", a=HEADS),
                                  P("causal")[0:HI, 0:HI].unsqueeze(1).to_broadcast([HI, HEADS, HI]),
                                  ALU.mult).then_inc(hi_masked, 1)

            def divide(b, p):
                dve.wait_ge(av_done, b + 1)
                dve.tensor_tensor(bcols(att, b), bank(6 + p, SEQ), bcols(rden, b), ALU.mult)\
                   .then_inc(att_ready, 1)

            masks(0, 0)
            masks(1, 1)
            divide(0, 0)
            with dve.Fori(1, GROUPS) as i:
                for p in range(2):
                    masks(i * 2 + p, p)
                    divide(i * 2 + (p - 1), 1 - p)
            divide(BATCH - 1, 1)

            dve.wait_ge(h_beta_ready, 1)
            with dve.Fori(0, GROUPS) as g:
                dve.wait_ge(ln2.rstd_ready, g + 1)
                dve.tensor_tensor(gcols(attn_x, g), gcols(centered, g), gcols(rstd, g),
                                  ALU.mult).then_inc(out_mul, 1)
                dve.wait_ge(out_mul, g + 1)
                dve.scalar_tensor_tensor(out=gcols(h1, g), in0=gcols(attn_x, g), scalar=P("attn_gamma"),
                                         in1=gcols(h_beta, g), op0=ALU.mult, op1=ALU.add).then_inc(h1_ready, 1)
            center(ln3, h1)
            normalize(ln3, xn)
            with dve.Fori(0, GROUPS) as g:
                dve.wait_ge(score_done, g + 1)
                dve.reduce_max(score_max[:, bass.ds(g * PER, PER)], gbank(g).rearrange("p (b l) -> p b l", b=PER),
                               axis=AX_X).then_inc(score_max_ready, 1)
            dve.wait_ge(score_max_ready, GROUPS)
            dve.tensor_scalar(score_shift[:], score_max[:], P("pool_b"), None, ALU.add)\
               .then_inc(score_shift_ready, 1)
            dve.wait_ge(score_shift_ready, 1)
            dve.tensor_scalar(score_bias[:], score_shift[:], -1.0, P("pool_b"), ALU.mult, ALU.add)\
               .then_inc(score_bias_ready, 1)
            dve.wait_ge(ln3.normed, GROUPS)
            with dve.Fori(0, BATCH) as b:
                dve.wait_ge(pool_exp_ready, b + 1)
                dve.scalar_tensor_tensor(out=bcols(attn_x, b), in0=bcols(xn, b), scalar=1.0, in1=bcols(pool_exp, b),
                                         op0=ALU.mult, op1=ALU.mult,
                                         accum_out=pooled_raw[:, bass.ds(b, 1)]).then_inc(pooled_step, 1)
            dve.reciprocal(exp_rsum[:], exp_sum[:]).then_inc(pooled_step, 1)
            dve.wait_ge(pooled_step, BATCH + 1)
            dve.tensor_tensor(pooled[:], pooled_raw[:], exp_rsum[:], ALU.mult).then_inc(pooled_ready, 1)

            dve.wait_ge(gate_done, 1)
            dve.tensor_tensor(gl[:, 0, :], bank(4, EXPERTS, slice(0, BATCH)), P("bias_gate")[0:BATCH, :], ALU.add)\
               .then_inc(gate_step, 1)
            dve.wait_ge(gate_step, 1)
            dve.tensor_reduce(gl[:, 1, 0:1], gl[:, 0, :], axis=AX_X, op=ALU.max, negate=True)\
               .then_inc(gate_step, 1)
            dve.wait_ge(gate_exp_ready, 1)
            dve.reciprocal(gl[:, 1, 2:3], gl[:, 1, 1:2]).then_inc(gate_step, 1)
            dve.wait_ge(gate_step, 3)
            dve.tensor_scalar(gl[:, 3, :], gl[:, 2, :], gl[:, 1, 2:3], None, ALU.mult).then_inc(gate_step, 1)
            dve.wait_ge(gate_step, 4)
            dve.max(gl[:, 4, :], gl[:, 3, :]).then_inc(gate_step, 1)
            dve.wait_ge(gate_step, 5)
            dve.max_index(gate_idx[:], gl[:, 4, :], gl[:, 3, :]).then_inc(gate_step, 1)
            dve.tensor_tensor(gl[:, 1, 3:4], gl[:, 4, 0:1], gl[:, 4, 1:2], ALU.add).then_inc(gate_step, 1)
            dve.wait_ge(gate_step, 7)
            dve.tensor_scalar(gl[:, 1, 4:5], gl[:, 1, 3:4], 1e-9, None, ALU.add).then_inc(gate_step, 1)
            dve.tensor_copy(gate_cat[:, 1, :], gate_idx[:, 0:TOP]).then_inc(gate_step, 1)
            dve.wait_ge(gate_step, 9)
            dve.reciprocal(gl[:, 1, 5:6], gl[:, 1, 4:5]).then_inc(gate_step, 1)
            dve.wait_ge(gate_step, 10)
            dve.tensor_scalar(gate_cat[:, 0, :], gl[:, 4, 0:TOP], gl[:, 1, 5:6], None, ALU.mult)\
               .then_inc(gate_step, 1)
            dve.wait_ge(gate_step, 11)
            for kind in range(2):
                dve.tensor_tensor(gate_rows[:, kind, :].rearrange("p (b s) -> p b s", s=TOP),
                                  P("diag")[0:BATCH, :].rearrange("p (b s) -> p b s", s=TOP),
                                  gate_cat[:, kind, :].unsqueeze(1).to_broadcast([BATCH, BATCH, TOP]),
                                  ALU.mult).then_inc(gate_rows_ready, 1)
            dve.wait_ge(gate_bcast_done, 1)
            dve.tensor_copy(gate_all[:], bank(5, UNITS)).then_inc(gates_ready, 1)
            dve.tensor_copy(expert_of[:], bank(5, UNITS, slice(0, 1), at=UNITS)).then_inc(gates_ready, 1)

            dve.wait_ge(gates_ready, 2)
            with dve.Fori(0, BATCH) as b:
                dve.wait_ge(eo_ready, b * 2 + 1)
                dve.scalar_tensor_tensor(out=acc[:], in0=eo[0][:], scalar=gate_all[:, bass.ds(b * 2, 1)],
                                         in1=bcols(h1, b), op0=ALU.mult, op1=ALU.add).then_inc(acc_ready, 1)
                dve.wait_ge(acc_ready, b * 2 + 1)
                dve.wait_ge(eo_ready, b * 2 + 2)
                dve.scalar_tensor_tensor(out=bcols(out_sb, b), in0=eo[1][:], scalar=gate_all[:, bass.ds(b * 2 + 1, 1)],
                                         in1=acc[:], op0=ALU.mult, op1=ALU.add).then_inc(acc_ready, 1)
                dve.wait_ge(acc_ready, b * 2 + 2)

        @block.tensor
        def _(pe):
            def mm(*args, **kw):
                return nc.tensor.matmul(*args, **kw)

            pe.wait_ge(patches_loaded, 32)
            for c in range(PATCH_CHUNKS):
                last = mm(bank(0, TOK_COLS), patch_w[:, c, :], patch_in[:, c, :], start=(c == 0),
                          stop=(c == PATCH_CHUNKS - 1))
            last.then_inc(embed_done, 1)
            pe.wait_ge(params_loaded, 16)
            pe.wait_ge(x_ready, 1)
            mm(bank(1, TOK_COLS), P("coord_spinor"), x_tok[:], start=True, stop=True).then_inc(coords_done, 1)
            pe.wait_ge(setup_vec, 4)
            pe.wait_ge(coord_spin_ready, 2)
            mm(bank(2, TOK_COLS), P("embed"), coord_spin[:], start=True, stop=True)
            mm(bank(3, TOK_COLS), P("spinor_sum"), coord_spin[:], start=True, stop=True)\
                .then_inc(manifold_done, 1)
            mm(bank(6, 1), P("ones_mean"), P("b_attn_out"), start=True, stop=True).then_inc(bias_mean_done, 1)
            pe.wait_ge(enh_ready, 1)
            mm(bank(4, TOK_COLS), P("ones_mean"), x_enh, start=True, stop=True).then_inc(tok_mean_done, 1)
            pe.wait_ge(tok_squared, 1)
            mm(bank(5, TOK_COLS), P("ones_mean"), tok_sq, start=True, stop=True).then_inc(tok_var_done, 1)
            pe.wait_ge(tok_normed, 1)
            mm(bank(7, TOK_COLS), P("tok_out"), tok_n, start=True, stop=True).then_inc(tok_out_done, 1)

            def stat(src, ready, k, done, per=1):
                with pe.Fori(0, GROUPS) as g:
                    if ready:
                        pe.wait_ge(ready, g * per + per)
                    mm(gbank(g, k), P("ones_mean"), gcols(src, g), start=True, stop=True).then_inc(done, 1)

            pe.wait_ge(text_loaded, 16)
            pe.wait_ge(tok_in_h, 1)
            stat(h, None, 0, ln1.mean_done)
            stat(squares, ln1.squared, 4, ln1.var_done)
            qkv = P("qkv")
            with pe.Fori(0, GROUPS) as g:
                pe.wait_ge(ln1.normed, g + 1)
                mm(gbank(g), qkv[:, 0:D], gcols(xn, g), start=True, stop=True).then_inc(q_done, 1)
                mm(gbank(g, 4), qkv[:, D:2 * D], gcols(xn, g), start=True, stop=True).then_inc(k_done, 1)
            with pe.Fori(0, GROUPS) as g:
                pe.wait_ge(qk_sum_ready, g + 1)
                mm(gbank(g), P("block_ones"), gcols(qk_sum, g), start=True, stop=True).then_inc(den_done, 1)

            def scores(b, p, first=False):
                pe.wait_ge(fix_ready, b * 2 + 2)
                if not first:
                    pe.wait_ge(v_ready, b * 4)
                mm(bank(5, D), x_fix[p][:, 0:LO], qkv[:, 2 * D:3 * D], start=True, stop=True)
                mm(bank(5, D, slice(0, HI), at=D), x_fix[p][:, LO:SEQ], qkv[:, 2 * D:3 * D], start=True,
                   stop=True).then_inc(v_done, 1)
                for pair in range(HEADS // 2):
                    if not first:
                        pe.wait_ge(lo_masked, b * 4 + (pair - 3))
                        pe.wait_ge(lo_copied, b * 4 + (pair - 3))
                    mm(bank(pair), k_fix[p][:, 0:LO], q_heads[:, 2 * pair:2 * pair + 2, bass.ds(b * SEQ, SEQ)],
                       start=True, stop=True).then_inc(lo_done, 1)
                if not first:
                    pe.wait_ge(hi_masked, b)
                mm(bank(4, HEADS * HI, slice(0, HI)), k_fix[p][:, LO:SEQ],
                   q_heads[:, :, bass.ds(b * SEQ + LO, HI)], start=True, stop=True).then_inc(hi_done, 1)

            def values(b, p):
                pe.wait_ge(v_ready, b * 4 + 4)
                pe.wait_ge(lo_masked, b * 4 + 4)
                pe.wait_ge(lo_copied, b * 4 + 4)
                pe.wait_ge(hi_masked, b + 1)
                if not isinstance(b, int) or b >= 2:
                    pe.wait_ge(att_ready, b - 1)
                for r in range(2):
                    for vals, scs, rows, at in ((v_lo[p], s_lo[p], 128, 0), (v_hi[p], s_hi[p], HI, LO)):
                        for j in range(HEADS // 2):
                            hd = 2 * j + r
                            last = mm(bank(6 + p, SEQ - at, slice(32 * j, 32 * j + 32), at=at),
                                      vals[0:rows, hd, :], scs[0:rows, hd, :],
                                      start=(r == 0 and at == 0), stop=(r == 1 and at > 0))
                last.then_inc(av_done, 1)

            pe.wait_ge(setup_vec, 11)
            pe.wait_ge(q_heads_loaded, 16 * HEADS * GROUPS)
            pe.wait_ge(den_ready, GROUPS)
            scores(0, 0, first=True)
            scores(1, 1)
            values(0, 0)
            with pe.Fori(1, GROUPS) as i:
                for p in range(2):
                    scores(i * 2 + p, p)
                    values(i * 2 + (p - 1), 1 - p)
            values(BATCH - 1, 1)

            pe.wait_ge(w_out_c_ready, 5)
            with pe.Fori(0, GROUPS) as g:
                pe.wait_ge(att_ready, g * 2 + 2)
                mm(gbank(g), w_out_c[:], gcols(att, g), start=True, stop=True).then_inc(out_done, 1)
            stat(squares, ln2.centered, 4, ln2.var_done, per=2)
            stat(h1, h1_ready, 0, ln3.mean_done)
            stat(squares, ln3.squared, 4, ln3.var_done)
            with pe.Fori(0, GROUPS) as g:
                pe.wait_ge(ln3.normed, g + 1)
                mm(gbank(g), pool_w128[:], gcols(xn, g), start=True, stop=True).then_inc(score_done, 1)
            pe.wait_ge(pooled_ready, 1)
            mm(bank(4, EXPERTS, slice(0, BATCH)), pooled[:], P("gate"), start=True, stop=True)\
                .then_inc(gate_done, 1)
            pe.wait_ge(gate_rows_ready, 2)
            mm(bank(5, 2 * UNITS), ones[0:BATCH, 0:128], gate_rows[:, :, :].rearrange("p k n -> p (k n)"),
               start=True, stop=True).then_inc(gate_bcast_done, 1)

            def up(u, k):
                pe.wait_ge(w_fixed, u + 1)
                if not isinstance(u, int) or u >= 2:
                    pe.wait_ge(hid_ready, u * 4 - 4)
                b = u // TOP
                for c in range(HID_CHUNKS):
                    last = mm(bank(2 * (k % 2) + c // 2, SEQ, at=(c % 2) * SEQ),
                              w_fix[k][:, W1_AT + 128 * c:W1_AT + 128 * (c + 1)], bcols(xn, b), start=True, stop=True)
                    if c % 2:
                        last.then_inc(up_done, 1)

            def down(u, k):
                pe.wait_ge(hid_ready, u * 4 + 4)
                if not isinstance(u, int) or u >= 2:
                    pe.wait_ge(eo_ready, u - 1)
                for c in range(HID_CHUNKS):
                    last = mm(bank(4 + k % 2, SEQ), w_fix[k][:, W2_AT + 128 * c:W2_AT + 128 * (c + 1)],
                              hid[k % 2][:, c, :], start=(c == 0), stop=(c == HID_CHUNKS - 1))
                last.then_inc(down_done, 1)

            up(0, 0)
            for k in range(3):
                up(k + 1, k + 1)
                down(k, k)
            with pe.Fori(1, UNITS // 4) as i:
                for k in range(4):
                    up(i * 4 + k, k)
                    down(i * 4 + (k - 1), (k + 3) % 4)
            down(UNITS - 1, 3)


def _param_array(t):
    prm = np.zeros((128, PARAM_COLS), np.float32)

    def put(name, a, row=0):
        at, n = AT[name]
        a = np.asarray(a, np.float32)
        a = a[:, None] if a.ndim == 1 else a
        prm[row:row + a.shape[0], at:at + a.shape[1]] = a

    at, _ = AT["coord_spinor"]
    put("coord_spinor", t["L0_tok_W_coord"])
    prm[:, at + SPINOR_AT:at + SPINOR_AT + SPINOR] = t["L0_tok_W_spinor"]
    put("embed", t["L0_tok_W_embed"])
    put("tok_out", t["L0_tok_W_out"])
    put("qkv", t["L0_attn_W_qkv"])
    put("attn_out", t["L0_attn_W_out"])
    put("gate", t["L0_ffn_gate_w"])
    put("bias_v", np.broadcast_to(t["L0_attn_b_qkv"][2 * D:], (128, D)))
    put("bias_gate", np.broadcast_to(t["L0_ffn_gate_b"], (128, EXPERTS)))
    put("pos", t["L0_tok_pos_embed"][0].T)
    put("ones_mean", np.full((128, D), 1.0 / D))
    put("spinor_sum", np.ones((SPINOR, D)), SPINOR_AT)
    head_of = np.arange(D) // HEAD
    put("block_ones", head_of[:, None] == head_of[None, :])
    put("causal", np.arange(LO)[None, :] >= np.arange(128)[:, None])
    put("position", np.broadcast_to(np.arange(SEQ), (128, SEQ)))
    put("diag", np.repeat(np.eye(BATCH), TOP, axis=1))
    put("b_patch", t["L0_tok_b_patch"])
    put("b_coord_spinor", t["L0_tok_b_coord"])
    put("b_coord_spinor", t["L0_tok_b_spinor"], SPINOR_AT)
    put("b_embed", t["L0_tok_b_embed"])
    put("tok_gamma", t["L0_tok_ln_gamma"])
    put("tok_beta", t["L0_tok_ln_beta"])
    put("b_tok_out", t["L0_tok_b_out"])
    put("b_q", t["L0_attn_b_qkv"][:D])
    put("b_k", t["L0_attn_b_qkv"][D:2 * D])
    put("b_attn_out", t["L0_attn_b_out"])
    put("decay", np.repeat(t["L0_attn_decay_logits"], HEAD))
    put("attn_gamma", t["L0_attn_ln_g"])
    put("attn_beta", t["L0_attn_ln_b"])
    put("pool_w", t["L0_ffn_attn_w"])
    put("pool_b", np.broadcast_to(t["L0_ffn_attn_b"], (128,)))
    return prm


def kernel(**inputs):
    import concourse.bacc as _bacc
    from concourse.bass_utils import run_bass_kernel_spmd as _run

    t = {k: np.asarray(v) for k, v in inputs.items()}
    patches = t["x"].reshape(BATCH, CHANNELS, GRID, PATCH, GRID, PATCH).transpose(1, 3, 5, 0, 2, 4)
    arrays = {
        "patches": patches.reshape(PATCH_CHUNKS, 128, TOK_COLS).transpose(1, 0, 2),
        "text": t["txt"].transpose(2, 0, 1),
        "w_patch": t["L0_tok_W_patch"].reshape(PATCH_CHUNKS, 128, D).transpose(1, 0, 2),
        "params": _param_array(t),
        "experts": np.concatenate([
            t["L0_ffn_w1"].transpose(1, 0, 2),
            t["L0_ffn_w2"].reshape(EXPERTS, HID_CHUNKS, 128, D).transpose(2, 0, 1, 3).reshape(128, EXPERTS, HIDDEN),
            t["L0_ffn_b1"].reshape(EXPERTS, HID_CHUNKS, 128).transpose(2, 0, 1),
            t["L0_ffn_b2"].T[:, :, None]], axis=2),
    }
    nc = _bacc.Bacc("TRN2", target_bir_lowering=False, num_devices=1)
    arrays = {k: np.ascontiguousarray(a) for k, a in arrays.items()}
    args = [nc.dram_tensor(k, a.shape, mybir.dt.from_np(a.dtype), kind="ExternalInput").ap()
            for k, a in arrays.items()]
    out = nc.dram_tensor("out", (D, COLS), F32, kind="ExternalOutput").ap()
    build(nc, *args, out)
    r = _run(nc, [arrays], core_ids=[0])
    return np.ascontiguousarray(r.results[0]["out"].reshape(D, BATCH, SEQ).transpose(1, 2, 0))
```

```python
from contextlib import ExitStack

import numpy as np

import concourse.bass as bass
from concourse import mybir

F32 = mybir.dt.float32
I32 = mybir.dt.int32
U32 = mybir.dt.uint32
ALU = mybir.AluOpType
ACT = mybir.ActivationFunctionType
AX_X = mybir.AxisListType.X

BATCH, CHANNELS, IMAGE, PATCH = 8, 3, 112, 16
GRID = IMAGE // PATCH
PATCHES = GRID * GRID
PATCH_DIM = CHANNELS * PATCH * PATCH
PATCH_CHUNKS = PATCH_DIM // 128
TEXT = 128
D = 128
COORDS, SPINOR = 8, 4
SPINOR_AT = 32
SEQ = PATCHES + TEXT
COLS = BATCH * SEQ
TOK_COLS = BATCH * PATCHES
HEADS = 8
HEAD = D // HEADS
EXPERTS, HIDDEN, TOP = 8, 512, 2
HID_CHUNKS = HIDDEN // 128
EPS = 1e-5

PER = 2
GROUPS = BATCH // PER
GC = PER * SEQ
BANK = 512
LO = 128
HI = SEQ - LO
UNITS = BATCH * TOP

MATS = [("coord_spinor", D), ("embed", D), ("tok_out", D), ("qkv", 3 * D), ("attn_out", D), ("gate", EXPERTS),
        ("bias_v", D), ("bias_gate", EXPERTS), ("pos", PATCHES),
        ("ones_mean", D), ("center", D), ("spinor_sum", D), ("block_ones", D), ("causal", LO), ("position", SEQ),
        ("diag", BATCH * TOP)]
VECS = ["b_patch", "b_coord_spinor", "b_embed", "tok_gamma", "tok_beta", "b_tok_out", "b_q", "b_k", "b_attn_out",
        "decay", "attn_gamma", "attn_beta", "pool_w", "pool_b"]
AT = {}
for _name, _n in MATS + [(_v, 1) for _v in VECS]:
    AT[_name] = (sum(n for _, n in AT.values()), _n)
PARAM_COLS = sum(n for _, n in AT.values())
W1_AT, W2_AT, B1_AT, B2_AT = 0, HIDDEN, 2 * HIDDEN, 2 * HIDDEN + HID_CHUNKS
EXPERT_COLS = B2_AT + 1


def build(nc, patches, text, w_patch, params, experts, out):
    ctx = ExitStack()
    with ctx:
        def sb(name, shape, dt=F32):
            return ctx.enter_context(nc.sbuf_tensor(name, shape, dt))

        def sem(name):
            return ctx.enter_context(nc.semaphore(name))

        prm = sb("prm", [128, PARAM_COLS])
        patch_in = sb("patch_in", [128, PATCH_CHUNKS, TOK_COLS])
        patch_w = sb("patch_w", [128, PATCH_CHUNKS, D])
        expert_w = sb("expert_w", [128, EXPERTS, EXPERT_COLS])
        x_tok = sb("x_tok", [128, TOK_COLS])
        coord_spin = sb("coord_spin", [128, TOK_COLS])
        manifold, x_enh, tok_sq, tok_log, tok_rstd, tok_n = [patch_in[:, n, :] for n in range(PATCH_CHUNKS)]
        h = sb("h", [128, COLS])
        h_beta = sb("h_beta", [128, COLS])
        xn = sb("xn", [128, COLS])
        q_dec = sb("q_dec", [128, COLS])
        k_dec = sb("k_dec", [128, COLS])
        k_sum = sb("k_sum", [128, COLS])
        qk_sum = sb("qk_sum", [128, COLS])
        den_log = k_sum
        rden = sb("rden", [128, COLS])
        att = sb("att", [128, COLS])
        sq1 = sb("sq1", [128, 3, BANK])
        rstd1 = sb("rstd1", [128, 3, BANK])
        q_exp = sb("q_exp", [128, 3, BANK])
        q_pos = sb("q_pos", [128, 3, BANK])
        k_exp = sb("k_exp", [128, 3, BANK])
        k_pos = sb("k_pos", [128, 3, BANK])
        q_heads = sb("q_heads", [128, HEADS, COLS])
        decay_q = sb("decay_q", [128, SEQ])
        decay_k = sb("decay_k", [128, SEQ])
        ones = sb("ones", [128, SEQ])
        lam = sb("lam", [128, 8])
        w_out_c = sb("w_out_c", [128, D])
        out_stat = sb("out_stat", [128, 4])
        pool_w128 = sb("pool_w128", [128, 128])
        eps_col = sb("eps_col", [128, 2])
        v_lo = [sb(f"v_lo{p}", [128, HEADS, 2 * HEAD]) for p in range(2)]
        v_hi = [sb(f"v_hi{p}", [128, HEADS, 2 * HEAD]) for p in range(2)]
        s_lo = [sb(f"s_lo{p}", [128, HEADS, SEQ]) for p in range(2)]
        s_hi = [sb(f"s_hi{p}", [HI, HEADS, HI]) for p in range(2)]
        sq2 = sq1[:, 0:2, 0:GC]
        rstd2 = rstd1[:, 0:2, 0:GC]
        attn_x = q_exp[:, 0:2, 0:GC]
        h1 = q_dec
        xn3 = k_sum
        pool_exp = qk_sum
        pool_prod = k_dec
        score_max = sb("score_max", [128, BATCH])
        score_shift = sb("score_shift", [128, BATCH])
        score_bias = sb("score_bias", [128, BATCH])
        exp_sum = sb("exp_sum", [128, BATCH])
        exp_rsum = sb("exp_rsum", [128, BATCH])
        pooled_raw = sb("pooled_raw", [128, BATCH])
        pooled = sb("pooled", [128, BATCH])
        gl = sb("gl", [PER, GROUPS, 5, EXPERTS])
        gate_idx = sb("gate_idx", [PER, GROUPS, EXPERTS], U32)
        gate_cat = sb("gate_cat", [PER, GROUPS, 2, TOP])
        gate_rows = sb("gate_rows", [PER, GROUPS, 2, PER * TOP])
        gate_all = sb("gate_all", [128, UNITS])
        expert_of = sb("expert_of", [1, UNITS], I32)
        w_fix = [q_heads[:, k, 0:EXPERT_COLS] for k in range(4)]
        hid = [q_heads[:, 4 + k, 0:HID_CHUNKS * SEQ].rearrange("p (c l) -> p c l", c=HID_CHUNKS) for k in range(2)]
        eo = [q_heads[:, 6, k * SEQ:(k + 1) * SEQ] for k in range(2)]
        acc = q_heads[:, 7, 0:SEQ]
        out_sb = rden
        ps = ctx.enter_context(nc.psum_tensor("ps", [128, 8 * BANK], F32))

        def P(name):
            at, n = AT[name]
            return prm[:, at:at + n]

        def bank(k, n=GC, rows=slice(0, 128), at=0):
            return ps[rows, k * BANK + at:k * BANK + at + n]

        def gcols(t, g):
            return t[:, g * GC:(g + 1) * GC]

        def bcols(t, b):
            return t[:, b * SEQ:(b + 1) * SEQ]

        def rcols(t, b):
            return t[:, bass.ds(b * SEQ, SEQ)]

        LO_A, LO_B, TAIL, HIGH, VALUE, AV, POST_X, POST_Y = range(8)

        def post_x(g):
            return VALUE if g == GROUPS - 1 else POST_X

        def post_y(g):
            return AV if g == GROUPS - 1 else POST_Y

        TEXT_A, TEXT_B, IMG = range(3)
        SET_COLS = (BATCH // 2 * TEXT, BATCH // 2 * TEXT, TOK_COLS)
        SET_BANKS = ((4, 5, 5, 4), (6, 7, 7, 6), (3, 0, 1, 2))

        def set_view(t, s):
            by_batch = t[:, :].rearrange("p (b l) -> p b l", b=BATCH)
            if s == IMG:
                return by_batch[:, :, 0:PATCHES]
            return by_batch[:, s * BATCH // 2:(s + 1) * BATCH // 2, PATCHES:SEQ]

        def shaped(flat, s):
            return flat.rearrange("p (b l) -> p b l", b=BATCH if s == IMG else BATCH // 2)

        def set_bank(s, which):
            return bank(SET_BANKS[s][which], SET_COLS[s])

        def dense(t, s):
            return t[:, s, 0:SET_COLS[s]]

        def set_decay(t, s):
            n = BATCH if s == IMG else BATCH // 2
            part = t[:, 0:PATCHES] if s == IMG else t[:, PATCHES:SEQ]
            return part.unsqueeze(1).to_broadcast([128, n, part.shape[1]])

        patch_w_loaded = sem("patch_w_loaded")
        patches_loaded = [sem(f"patches_loaded{n}") for n in range(3)]
        text_b_loaded = sem("text_b_loaded")
        experts_loaded = sem("experts_loaded")
        q_heads_zeroed = sem("q_heads_zeroed")
        q_dec_ready = [sem(f"q_dec_ready{n}") for n in range(3)]
        q_heads_loaded = [sem(f"q_heads_loaded{n}") for n in range(4)]
        acc_ready = sem("acc_ready")
        out_stored = sem("out_stored")
        decay_ready = sem("decay_ready")
        q_elu_ready = sem("q_elu_ready")
        k_elu_ready = sem("k_elu_ready")
        k_dec_ready = sem("k_dec_ready")
        k_sum_ready = sem("k_sum_ready")
        qk_sum_ready = sem("qk_sum_ready")
        text_a_loaded = sem("text_a_loaded")
        tok_in_h = sem("tok_in_h")
        params_loaded = sem("params_loaded")
        h_beta_ready = sem("h_beta_ready")
        setup_act = sem("setup_act")
        ln1_centered = [sem(f"ln1_centered{n}") for n in range(3)]
        ln1_squared = [sem(f"ln1_squared{n}") for n in range(3)]
        ln1_var_done = [sem(f"ln1_var_done{n}") for n in range(3)]
        ln1_log = [sem(f"ln1_log{n}") for n in range(3)]
        ln1_rstd_ready = [sem(f"ln1_rstd_ready{n}") for n in range(3)]
        q_done = [sem(f"q_done{n}") for n in range(3)]
        q_parts_ready = [sem(f"q_parts_ready{n}") for n in range(3)]
        k_done = [sem(f"k_done{n}") for n in range(3)]
        k_exp_ready = [sem(f"k_exp_ready{n}") for n in range(3)]
        setup_vec = sem("setup_vec")
        coords_done = sem("coords_done")
        coord_spin_ready = sem("coord_spin_ready")
        manifold_done = sem("manifold_done")
        manifold_ready = sem("manifold_ready")
        tok_centered = sem("tok_centered")
        tok_squared = sem("tok_squared")
        tok_var_done = sem("tok_var_done")
        tok_log_ready = sem("tok_log_ready")
        tok_rstd_ready = sem("tok_rstd_ready")
        den_done = sem("den_done")
        den_log_ready = sem("den_log_ready")
        rden_ready = sem("rden_ready")
        tail_done = sem("tail_done")
        av_done = sem("av_done")
        tail_copied = sem("tail_copied")
        out_done = sem("out_done")
        out_squared = sem("out_squared")
        out_var_done = sem("out_var_done")
        out_log = sem("out_log")
        out_rstd_ready = sem("out_rstd_ready")
        h1_centered = sem("h1_centered")
        h1_squared = sem("h1_squared")
        h1_var_done = sem("h1_var_done")
        h1_log = sem("h1_log")
        h1_rstd_ready = sem("h1_rstd_ready")
        score_bias_ready = sem("score_bias_ready")
        pool_exp_ready = sem("pool_exp_ready")
        gate_shift_ready = sem("gate_shift_ready")
        gate_exp_ready = sem("gate_exp_ready")
        down_done = sem("down_done")
        up_done = sem("up_done")
        hid_ready = sem("hid_ready")
        eo_ready = sem("eo_ready")
        v_zeroed = sem("v_zeroed")
        w_out_step = sem("w_out_step")
        embed_done = sem("embed_done")
        x_ready = sem("x_ready")
        ln1_normed = [sem(f"ln1_normed{n}") for n in range(3)]
        k_pos_ready = sem("k_pos_ready")
        enh_mul = sem("enh_mul")
        enh_ready = sem("enh_ready")
        tok_mul = sem("tok_mul")
        tok_normed = sem("tok_normed")
        tok_out_done = sem("tok_out_done")
        v_done = sem("v_done")
        v_ready = sem("v_ready")
        lo_done = sem("lo_done")
        lo_masked = sem("lo_masked")
        high_done = sem("high_done")
        high_masked = sem("high_masked")
        att_ready = sem("att_ready")
        h1_ready = sem("h1_ready")
        out_mul = sem("out_mul")
        h1_normed = sem("h1_normed")
        score_done = sem("score_done")
        score_max_ready = sem("score_max_ready")
        score_shift_ready = sem("score_shift_ready")
        pooled_step = sem("pooled_step")
        pooled_ready = sem("pooled_ready")
        gate_done = sem("gate_done")
        gate_logits_ready = sem("gate_logits_ready")
        gate_step = sem("gate_step")
        gate_rows_ready = sem("gate_rows_ready")
        gate_bcast_done = sem("gate_bcast_done")
        gates_ready = sem("gates_ready")
        w_fixed = sem("w_fixed")

        block = ctx.enter_context(nc.Block())

        @block.sync
        def _(sp):
            sp.dma_start(patch_w[:], w_patch).then_inc(patch_w_loaded, 16)
            for c in range(3):
                sp.dma_start(patch_in[:, 2 * c:2 * c + 2, :], patches[:, 2 * c:2 * c + 2, :])\
                    .then_inc(patches_loaded[c], 16)
            sp.wait_ge(text_b_loaded, 16)
            sp.dma_start(expert_w[:], experts).then_inc(experts_loaded, 16)
            sp.wait_ge(q_heads_zeroed, 1)
            half = COLS // 2
            for n in range(2):
                sp.wait_ge(q_dec_ready[n], 1)
                sp.wait_ge(q_dec_ready[IMG], 1)
                for hd in range(HEADS):
                    rows = slice(HEAD * hd, HEAD * hd + HEAD)
                    sp.dma_start(q_heads[rows, hd, n * half:(n + 1) * half], q_dec[rows, n * half:(n + 1) * half])\
                        .then_inc(q_heads_loaded[2 * n + hd // 4], 16)
            with sp.Fori(0, BATCH) as b:
                at = sp.snap(b * SEQ)
                added = sp.snap(b * TOP + TOP)
                sp.wait_ge(acc_ready, added)
                sp.dma_start(out[:, bass.ds(at, SEQ)], out_sb[:, bass.ds(at, SEQ)]).then_inc(out_stored, 16)
            sp.wait_ge(out_stored, 16 * BATCH)

        @block.gpsimd
        def _(pool):
            nc.gpsimd.memset(q_heads[:], 0.0).then_inc(q_heads_zeroed, 1)

            pool.wait_ge(decay_ready, 3)
            for s in (TEXT_A, TEXT_B):
                pool.wait_ge(q_elu_ready, s + 1)
                nc.gpsimd.tensor_tensor(set_view(q_dec, s), shaped(dense(q_pos, s), s), set_decay(decay_q, s),
                                        ALU.mult).then_inc(q_dec_ready[s], 1)
                pool.wait_ge(k_elu_ready, s + 1)
                nc.gpsimd.tensor_tensor(set_view(k_dec, s), shaped(dense(k_pos, s), s), set_decay(decay_k, s),
                                        ALU.mult).then_inc(k_dec_ready, 1)
            for g in range(GROUPS):
                pool.wait_ge(k_sum_ready, PER * (g + 1))
                nc.gpsimd.tensor_tensor(gcols(qk_sum, g), gcols(q_dec, g), gcols(k_sum, g),
                                        ALU.mult).then_inc(qk_sum_ready, 1)
            pool.wait_ge(text_a_loaded, 16)
            pool.wait_ge(text_b_loaded, 16)
            pool.wait_ge(tok_in_h, 1)
            pool.wait_ge(params_loaded, 16)
            nc.gpsimd.tensor_scalar(h_beta[:], h[:], P("attn_beta"), None, ALU.add).then_inc(h_beta_ready, 1)

        @block.scalar
        def _(act):
            nc.scalar.dma_start(prm[:], params).then_inc(params_loaded, 16)
            nc.scalar.dma_start(set_view(h, TEXT_A), text[:, 0:BATCH // 2, :]).then_inc(text_a_loaded, 16)
            nc.scalar.dma_start(set_view(h, TEXT_B), text[:, BATCH // 2:BATCH, :]).then_inc(text_b_loaded, 16)
            nc.scalar.preload_act_table_set("natural_log_exp_and_others")
            act.wait_ge(params_loaded, 16)
            nc.scalar.activation(lam[:, 0:1], P("decay"), ACT.Exp, scale=-1.0).then_inc(setup_act, 1)

            def square_of_set(s):
                act.wait_ge(ln1_centered[s], 1)
                nc.scalar.activation(dense(sq1, s), set_bank(s, 0), ACT.Square).then_inc(ln1_squared[s], 1)

            def rstd_of_set(s):
                act.wait_ge(ln1_var_done[s], 1)
                nc.scalar.activation(dense(sq1, s), set_bank(s, 1), ACT.Ln, bias=eps_col[:, 0:1])\
                    .then_inc(ln1_log[s], 1)
                act.wait_ge(ln1_log[s], 1)
                nc.scalar.activation(dense(rstd1, s), dense(sq1, s), ACT.Exp, scale=-0.5)\
                    .then_inc(ln1_rstd_ready[s], 1)

            def elu_parts(s):
                act.wait_ge(q_done[s], 1)
                nc.scalar.activation(dense(q_exp, s), set_bank(s, 2), ACT.Exp, bias=P("b_q"))\
                    .then_inc(q_parts_ready[s], 1)
                nc.scalar.activation(dense(q_pos, s), set_bank(s, 2), ACT.Relu, bias=P("b_q"))\
                    .then_inc(q_parts_ready[s], 1)
                act.wait_ge(k_done[s], 1)
                nc.scalar.activation(dense(k_exp, s), set_bank(s, 3), ACT.Exp, bias=P("b_k"))\
                    .then_inc(k_exp_ready[s], 1)

            act.wait_ge(setup_vec, 7)
            nc.scalar.activation(lam[:, 4:5], lam[:, 3:4], ACT.Ln).then_inc(setup_act, 1)
            act.wait_ge(setup_act, 2)
            nc.scalar.mul(lam[:, 5:6], lam[:, 4:5], -1.0).then_inc(setup_act, 1)
            act.wait_ge(setup_act, 3)
            nc.scalar.activation(decay_q[:], P("position"), ACT.Exp, scale=lam[:, 4:5]).then_inc(decay_ready, 1)
            nc.scalar.activation(decay_k[:], P("position"), ACT.Exp, scale=lam[:, 5:6]).then_inc(decay_ready, 1)
            square_of_set(TEXT_A)
            square_of_set(TEXT_B)
            act.wait_ge(coords_done, 1)
            nc.scalar.activation(coord_spin[0:COORDS, :], bank(1, TOK_COLS, slice(0, COORDS)), ACT.Identity,
                                 bias=P("b_coord_spinor")[0:COORDS, :]).then_inc(coord_spin_ready, 1)
            sp_rows = slice(SPINOR_AT, SPINOR_AT + SPINOR)
            nc.scalar.activation(coord_spin[sp_rows, :], bank(1, TOK_COLS, sp_rows), ACT.Square,
                                 bias=P("b_coord_spinor")[sp_rows, :]).then_inc(coord_spin_ready, 1)
            rstd_of_set(TEXT_A)
            act.wait_ge(manifold_done, 1)
            nc.scalar.activation(manifold, bank(2, TOK_COLS), ACT.Identity,
                                 bias=P("b_embed")).then_inc(manifold_ready, 1)
            rstd_of_set(TEXT_B)
            act.wait_ge(tok_centered, 1)
            nc.scalar.activation(tok_sq, bank(0, TOK_COLS), ACT.Square).then_inc(tok_squared, 1)
            elu_parts(TEXT_A)
            act.wait_ge(tok_var_done, 1)
            nc.scalar.activation(tok_log, bank(1, TOK_COLS), ACT.Ln, bias=eps_col[:, 0:1]).then_inc(tok_log_ready, 1)
            act.wait_ge(tok_log_ready, 1)
            nc.scalar.activation(tok_rstd, tok_log, ACT.Exp, scale=-0.5).then_inc(tok_rstd_ready, 1)
            elu_parts(TEXT_B)
            square_of_set(IMG)
            rstd_of_set(IMG)
            elu_parts(IMG)

            def den_reciprocal(g):
                act.wait_ge(den_done, g + 1)
                nc.scalar.activation(gcols(den_log, g), bank(POST_X + g % 2), ACT.Ln, bias=eps_col[:, 1:2])\
                    .then_inc(den_log_ready, 1)
                act.wait_ge(den_log_ready, g + 1)
                nc.scalar.activation(gcols(rden, g), gcols(den_log, g), ACT.Exp, scale=-1.0)\
                    .then_inc(rden_ready, 1)

            def copy_tail(b):
                act.wait_ge(tail_done, b + 1)
                if b >= 2:
                    act.wait_ge(av_done, b - 1)
                nc.scalar.activation(s_lo[b % 2][:, :, LO:SEQ],
                                     bank(TAIL, HEADS * HI).rearrange("p (a l) -> p a l", a=HEADS),
                                     ACT.Copy).then_inc(tail_copied, 1)

            def square_out(g):
                act.wait_ge(out_done, g + 1)
                nc.scalar.activation(sq2[:, g % 2, :], bank(post_x(g)), ACT.Square, bias=out_stat[:, 3:4])\
                    .then_inc(out_squared, 1)

            def rstd_out(g):
                act.wait_ge(out_var_done, g + 1)
                nc.scalar.activation(sq2[:, g % 2, :], bank(post_y(g)), ACT.Ln, bias=eps_col[:, 0:1])\
                    .then_inc(out_log, 1)
                act.wait_ge(out_log, g + 1)
                nc.scalar.activation(rstd2[:, g % 2, :], sq2[:, g % 2, :], ACT.Exp, scale=-0.5)\
                    .then_inc(out_rstd_ready, 1)

            def square_h1(g):
                act.wait_ge(h1_centered, g + 1)
                nc.scalar.activation(sq2[:, g % 2, :], bank(post_x(g)), ACT.Square).then_inc(h1_squared, 1)

            def rstd_h1(g):
                act.wait_ge(h1_var_done, g + 1)
                nc.scalar.activation(sq2[:, g % 2, :], bank(post_y(g)), ACT.Ln, bias=eps_col[:, 0:1])\
                    .then_inc(h1_log, 1)
                act.wait_ge(h1_log, g + 1)
                nc.scalar.activation(rstd2[:, g % 2, :], sq2[:, g % 2, :], ACT.Exp, scale=-0.5)\
                    .then_inc(h1_rstd_ready, 1)

            def exp_pool(g):
                act.wait_ge(score_bias_ready, g + 1)
                for b in (PER * g, PER * g + 1):
                    nc.scalar.activation(bcols(pool_exp, b), bank(post_x(g), SEQ, at=(b % PER) * SEQ), ACT.Exp,
                                         bias=score_bias[:, b:b + 1], accum_out=exp_sum[:, b:b + 1])\
                        .then_inc(pool_exp_ready, 1)

            def exp_gate(g):
                act.wait_ge(gate_shift_ready, g + 1)
                nc.scalar.activation(gl[:, g, 2, :], gl[:, g, 0, :], ACT.Exp, bias=gl[:, g, 1, 0:1],
                                     accum_out=gl[:, g, 1, 1:2]).then_inc(gate_exp_ready, 1)

            den_reciprocal(0)
            den_reciprocal(1)
            for b in range(BATCH):
                g = b // 2
                if b % 2 == 0:
                    if g >= 2:
                        rstd_h1(g - 2)
                    copy_tail(b)
                    if g >= 3:
                        exp_gate(g - 3)
                    if g >= 2:
                        exp_pool(g - 2)
                    if b == 0:
                        den_reciprocal(2)
                        den_reciprocal(3)
                else:
                    if g >= 1:
                        square_out(g - 1)
                        rstd_out(g - 1)
                    copy_tail(b)
                    if g >= 1:
                        square_h1(g - 1)
            last = GROUPS - 1
            rstd_h1(last - 1)
            square_out(last)
            exp_gate(last - 2)
            rstd_out(last)
            exp_pool(last - 1)
            square_h1(last)
            exp_gate(last - 1)
            rstd_h1(last)
            exp_pool(last)
            exp_gate(last)
            nc.scalar.preload_act_table(ACT.Gelu)

            def gelu_hidden(u, k):
                if not isinstance(u, int) or u >= 2:
                    act.wait_ge(down_done, u - 1)
                for c in range(HID_CHUNKS):
                    if c % 2 == 0:
                        act.wait_ge(up_done, u * 2 + (c // 2 + 1))
                    nc.scalar.activation(hid[k % 2][:, c, :], bank(2 * (k % 2) + c // 2, SEQ, at=(c % 2) * SEQ),
                                         ACT.Gelu, bias=w_fix[k][:, B1_AT + c:B1_AT + c + 1]).then_inc(hid_ready, 1)

            def gelu_out(u, k):
                act.wait_ge(down_done, u + 1)
                if not isinstance(u, int) or u >= 2:
                    act.wait_ge(acc_ready, u - 1)
                nc.scalar.activation(eo[k % 2], bank(4 + k % 2, SEQ), ACT.Gelu,
                                     bias=w_fix[k][:, B2_AT:B2_AT + 1]).then_inc(eo_ready, 1)

            gelu_hidden(0, 0)
            for k in range(3):
                gelu_hidden(k + 1, k + 1)
                gelu_out(k, k)
            with act.Fori(1, UNITS // 4) as i:
                for k in range(4):
                    gelu_hidden(i * 4 + k, k)
                    gelu_out(i * 4 + (k - 1), (k + 3) % 4)
            gelu_out(UNITS - 1, 3)

        @block.vector
        def _(dve):
            dve.memset(eps_col[:, 0:1], EPS).then_inc(setup_vec, 1)
            dve.memset(eps_col[:, 1:2], 1e-6).then_inc(setup_vec, 1)
            dve.memset(ones[:], 1.0).then_inc(setup_vec, 1)
            dve.memset(coord_spin[:], 0.0).then_inc(setup_vec, 1)
            for p in range(2):
                dve.memset(v_lo[p][:], 0.0).then_inc(v_zeroed, 1)
                dve.memset(v_hi[p][:], 0.0).then_inc(v_zeroed, 1)
            dve.wait_ge(setup_act, 1)
            dve.tensor_scalar(lam[:, 1:2], lam[:, 0:1], 1.0, None, ALU.add).then_inc(setup_vec, 1)
            dve.wait_ge(setup_vec, 5)
            dve.reciprocal(lam[:, 2:3], lam[:, 1:2]).then_inc(setup_vec, 1)
            dve.wait_ge(setup_vec, 6)
            dve.tensor_scalar(lam[:, 3:4], lam[:, 2:3], 0.01, 0.99, ALU.mult, ALU.add).then_inc(setup_vec, 1)
            dve.reduce_sum(out_stat[:, 0:1], P("attn_out"), axis=AX_X).then_inc(w_out_step, 1)
            dve.tensor_scalar(pool_w128[:], ones[:, 0:128], P("pool_w"), None, ALU.mult).then_inc(w_out_step, 1)
            dve.wait_ge(w_out_step, 2)
            dve.tensor_scalar(out_stat[:, 1:2], out_stat[:, 0:1], 1.0 / D, None, ALU.mult).then_inc(w_out_step, 1)
            dve.wait_ge(w_out_step, 3)
            dve.tensor_scalar(w_out_c[:], P("attn_out"), out_stat[:, 1:2], None, ALU.subtract).then_inc(w_out_step, 1)
            dve.wait_ge(decay_ready, 2)
            dve.tensor_scalar(decay_q[:], decay_q[:], float(HEAD) ** -0.5, None, ALU.mult).then_inc(decay_ready, 1)
            dve.wait_ge(embed_done, 1)
            dve.scalar_tensor_tensor(
                out=x_tok[:, :].rearrange("p (b n) -> p b n", b=BATCH),
                in0=bank(0, TOK_COLS).rearrange("p (b n) -> p b n", b=BATCH), scalar=P("b_patch"),
                in1=P("pos").unsqueeze(1).to_broadcast([128, BATCH, PATCHES]),
                op0=ALU.add, op1=ALU.add).then_inc(x_ready, 1)

            def normalize_set(s):
                dve.wait_ge(ln1_rstd_ready[s], 1)
                dve.tensor_tensor(set_view(xn, s), shaped(set_bank(s, 0), s), shaped(dense(rstd1, s), s),
                                  ALU.mult).then_inc(ln1_normed[s], 1)

            def elu_q(s):
                dve.wait_ge(q_parts_ready[s], 2)
                dve.scalar_tensor_tensor(out=dense(q_pos, s), in0=dense(q_exp, s), scalar=1.0, in1=dense(q_pos, s),
                                         op0=ALU.min, op1=ALU.add).then_inc(q_elu_ready, 1)

            def elu_k(s):
                dve.wait_ge(k_exp_ready[s], 1)
                dve.tensor_scalar(dense(k_pos, s), set_bank(s, 3), P("b_k"), 0.0, ALU.add, ALU.max)\
                    .then_inc(k_pos_ready, 1)
                dve.wait_ge(k_pos_ready, s + 1)
                dve.scalar_tensor_tensor(out=dense(k_pos, s), in0=dense(k_exp, s), scalar=1.0, in1=dense(k_pos, s),
                                         op0=ALU.min, op1=ALU.add).then_inc(k_elu_ready, 1)

            normalize_set(TEXT_A)
            dve.wait_ge(manifold_ready, 1)
            dve.tensor_tensor(manifold, manifold, bank(3, TOK_COLS), ALU.mult).then_inc(enh_mul, 1)
            dve.wait_ge(enh_mul, 1)
            dve.tensor_tensor(x_enh, manifold, x_tok[:], ALU.add).then_inc(enh_ready, 1)
            normalize_set(TEXT_B)
            dve.wait_ge(manifold_done, 1)
            dve.tensor_tensor(out_stat[:, 3:4], P("b_attn_out"), bank(3, 1, at=TOK_COLS), ALU.subtract)\
                .then_inc(w_out_step, 1)
            elu_q(TEXT_A)
            elu_k(TEXT_A)
            dve.wait_ge(tok_rstd_ready, 1)
            dve.scalar_tensor_tensor(out=tok_n, in0=bank(0, TOK_COLS), scalar=P("tok_gamma"), in1=tok_rstd,
                                     op0=ALU.mult, op1=ALU.mult).then_inc(tok_mul, 1)
            dve.wait_ge(tok_mul, 1)
            dve.tensor_scalar(tok_n, tok_n, P("tok_beta"), None, ALU.add).then_inc(tok_normed, 1)
            dve.wait_ge(tok_out_done, 1)
            dve.tensor_scalar(set_view(h, IMG), shaped(bank(2, TOK_COLS), IMG), P("b_tok_out"), None,
                              ALU.add).then_inc(tok_in_h, 1)
            elu_q(TEXT_B)
            elu_k(TEXT_B)
            normalize_set(IMG)
            elu_q(IMG)
            dve.wait_ge(q_elu_ready, IMG + 1)
            dve.tensor_tensor(set_view(q_dec, IMG), shaped(dense(q_pos, IMG), IMG), set_decay(decay_q, IMG),
                              ALU.mult).then_inc(q_dec_ready[IMG], 1)
            elu_k(IMG)
            dve.wait_ge(k_elu_ready, IMG + 1)
            dve.tensor_tensor(set_view(k_dec, IMG), shaped(dense(k_pos, IMG), IMG), set_decay(decay_k, IMG),
                              ALU.mult).then_inc(k_dec_ready, 1)
            dve.wait_ge(k_dec_ready, 3)
            for b in range(BATCH):
                dve.tensor_tensor_scan(bcols(k_sum, b), ones[:], bcols(k_dec, b), 0.0,
                                       ALU.mult, ALU.add).then_inc(k_sum_ready, 1)

            def add_value_bias(b):
                dve.wait_ge(v_done, b + 1)
                if b >= 2:
                    dve.wait_ge(av_done, b - 1)
                for rows, at, dst in ((128, 0, v_lo[b % 2]), (HI, D, v_hi[b % 2])):
                    halves = dst[0:rows, :, :].rearrange("p (j r) (a c) -> p j (r a) c", r=2, a=2)[:, :, 0:4:3, :]
                    dve.tensor_tensor(
                        halves,
                        bank(VALUE, D, slice(0, rows), at).rearrange("p (j r c) -> p j r c", r=2, c=HEAD),
                        P("bias_v")[0:rows, :].rearrange("p (j r c) -> p j r c", r=2, c=HEAD),
                        ALU.add).then_inc(v_ready, 1)

            def mask_lo(b, n):
                dve.wait_ge(lo_done, 2 * b + n + 1)
                dve.tensor_tensor(s_lo[b % 2][:, 4 * n:4 * n + 4, 0:LO],
                                  bank(LO_A + n, 4 * LO).rearrange("p (a l) -> p a l", a=4),
                                  P("causal").unsqueeze(1).to_broadcast([128, 4, LO]),
                                  ALU.mult).then_inc(lo_masked, 1)

            def mask_high(b):
                dve.wait_ge(high_done, b + 1)
                dve.tensor_tensor(s_hi[b % 2][:],
                                  bank(HIGH, HEADS * HI, slice(0, HI)).rearrange("p (a l) -> p a l", a=HEADS),
                                  P("causal")[0:HI, 0:HI].unsqueeze(1).to_broadcast([HI, HEADS, HI]),
                                  ALU.mult).then_inc(high_masked, 1)

            def divide(b):
                dve.wait_ge(rden_ready, b // PER + 1)
                dve.wait_ge(av_done, b + 1)
                dve.tensor_tensor(bcols(att, b), bank(AV, SEQ), bcols(rden, b), ALU.mult).then_inc(att_ready, 1)

            def residual(g):
                dve.wait_ge(out_rstd_ready, g + 1)
                if g >= 2:
                    dve.wait_ge(h1_ready, g - 1)
                dve.scalar_tensor_tensor(out=attn_x[:, g % 2, :], in0=bank(post_x(g)), scalar=out_stat[:, 3:4],
                                         in1=rstd2[:, g % 2, :], op0=ALU.add, op1=ALU.mult).then_inc(out_mul, 1)
                dve.wait_ge(h_beta_ready, 1)
                dve.wait_ge(out_mul, g + 1)
                dve.scalar_tensor_tensor(out=gcols(h1, g), in0=attn_x[:, g % 2, :], scalar=P("attn_gamma"),
                                         in1=gcols(h_beta, g), op0=ALU.mult, op1=ALU.add).then_inc(h1_ready, 1)

            def normalize_h1(g):
                dve.wait_ge(h1_rstd_ready, g + 1)
                dve.tensor_tensor(gcols(xn3, g), bank(post_x(g)), rstd2[:, g % 2, :], ALU.mult).then_inc(h1_normed, 1)

            def score_shifts(g):
                two = slice(PER * g, PER * g + PER)
                dve.wait_ge(score_done, g + 1)
                dve.reduce_max(score_max[:, two], bank(post_x(g)).rearrange("p (b l) -> p b l", b=PER),
                               axis=AX_X).then_inc(score_max_ready, 1)
                dve.wait_ge(score_max_ready, g + 1)
                dve.tensor_scalar(score_shift[:, two], score_max[:, two], P("pool_b"), None, ALU.add)\
                    .then_inc(score_shift_ready, 1)
                dve.wait_ge(score_shift_ready, g + 1)
                dve.tensor_scalar(score_bias[:, two], score_shift[:, two], -1.0, P("pool_b"), ALU.mult, ALU.add)\
                    .then_inc(score_bias_ready, 1)

            def pool_group(g):
                two = slice(PER * g, PER * g + PER)
                for b in (PER * g, PER * g + 1):
                    dve.wait_ge(pool_exp_ready, b + 1)
                    dve.scalar_tensor_tensor(out=bcols(pool_prod, b), in0=bcols(xn3, b), scalar=1.0,
                                             in1=bcols(pool_exp, b), op0=ALU.mult, op1=ALU.mult,
                                             accum_out=pooled_raw[:, b:b + 1]).then_inc(pooled_step, 1)
                dve.reciprocal(exp_rsum[:, two], exp_sum[:, two]).then_inc(pooled_step, 1)
                dve.wait_ge(pooled_step, 3 * (g + 1))
                dve.tensor_tensor(pooled[:, two], pooled_raw[:, two], exp_rsum[:, two], ALU.mult)\
                    .then_inc(pooled_ready, 1)

            def gate_logits(g):
                dve.wait_ge(gate_done, g + 1)
                dve.tensor_tensor(gl[:, g, 0, :], bank(post_y(g), EXPERTS, slice(0, PER)), P("bias_gate")[0:PER, :],
                                  ALU.add).then_inc(gate_logits_ready, 1)
                dve.wait_ge(gate_logits_ready, g + 1)
                dve.tensor_reduce(gl[:, g, 1, 0:1], gl[:, g, 0, :], axis=AX_X, op=ALU.max, negate=True)\
                    .then_inc(gate_shift_ready, 1)

            def gate_top(g):
                n = 8 * g
                row = gl[:, g, 1, :]
                dve.wait_ge(gate_exp_ready, g + 1)
                dve.reciprocal(row[:, 2:3], row[:, 1:2]).then_inc(gate_step, 1)
                dve.wait_ge(gate_step, n + 1)
                dve.tensor_scalar(gl[:, g, 3, :], gl[:, g, 2, :], row[:, 2:3], None, ALU.mult).then_inc(gate_step, 1)
                dve.wait_ge(gate_step, n + 2)
                dve.max(gl[:, g, 4, :], gl[:, g, 3, :]).then_inc(gate_step, 1)
                dve.wait_ge(gate_step, n + 3)
                dve.max_index(gate_idx[:, g, :], gl[:, g, 4, :], gl[:, g, 3, :]).then_inc(gate_step, 1)
                dve.scalar_tensor_tensor(out=row[:, 3:4], in0=gl[:, g, 4, 0:1], scalar=1e-9, in1=gl[:, g, 4, 1:2],
                                         op0=ALU.add, op1=ALU.add).then_inc(gate_step, 1)
                dve.wait_ge(gate_step, n + 5)
                dve.tensor_copy(gate_cat[:, g, 1, :], gate_idx[:, g, 0:TOP]).then_inc(gate_step, 1)
                dve.reciprocal(row[:, 4:5], row[:, 3:4]).then_inc(gate_step, 1)
                dve.wait_ge(gate_step, n + 7)
                dve.tensor_scalar(gate_cat[:, g, 0, :], gl[:, g, 4, 0:TOP], row[:, 4:5], None, ALU.mult)\
                    .then_inc(gate_step, 1)
                dve.wait_ge(gate_step, n + 8)
                for kind in range(2):
                    dve.tensor_tensor(gate_rows[:, g, kind, :].rearrange("p (b s) -> p b s", s=TOP),
                                      P("diag")[0:PER, 0:PER * TOP].rearrange("p (b s) -> p b s", s=TOP),
                                      gate_cat[:, g, kind, :].unsqueeze(1).to_broadcast([PER, PER, TOP]),
                                      ALU.mult).then_inc(gate_rows_ready, 1)

            def keep_gates(g):
                n = PER * TOP
                dve.wait_ge(gate_bcast_done, g + 1)
                dve.tensor_copy(gate_all[:, g * n:(g + 1) * n], bank(post_y(g), n)).then_inc(gates_ready, 1)
                dve.tensor_copy(expert_of[:, g * n:(g + 1) * n], bank(post_y(g), n, slice(0, 1), at=n))\
                    .then_inc(gates_ready, 1)

            dve.wait_ge(v_zeroed, 4)
            for b in range(BATCH):
                g = b // 2
                add_value_bias(b)
                if b % 2 == 1 and g >= 3:
                    keep_gates(g - 3)
                if b % 2 == 1 and g >= 2:
                    pool_group(g - 2)
                mask_lo(b, 0)
                mask_lo(b, 1)
                if b % 2 == 0 and g >= 3:
                    gate_logits(g - 3)
                mask_high(b)
                if b % 2 == 0:
                    if g >= 2:
                        normalize_h1(g - 2)
                    if b >= 1:
                        divide(b - 1)
                    if g >= 3:
                        gate_top(g - 3)
                    if g >= 2:
                        score_shifts(g - 2)
                else:
                    if g >= 1:
                        residual(g - 1)
                    divide(b - 1)
            last = GROUPS - 1
            divide(BATCH - 1)
            gate_logits(last - 2)
            normalize_h1(last - 1)
            gate_top(last - 2)
            score_shifts(last - 1)
            residual(last)
            keep_gates(last - 2)
            pool_group(last - 1)
            gate_logits(last - 1)
            gate_top(last - 1)

            def fetch(u, k):
                if not isinstance(u, int) or u >= 4:
                    dve.wait_ge(eo_ready, u - 3)
                e = dve.value_load(expert_of[0:1, bass.ds(u, 1)], min_val=0, max_val=EXPERTS - 1)
                dve.tensor_copy(w_fix[k], expert_w[:, bass.ds(e, 1), :].rearrange("p a n -> p (a n)"))\
                    .then_inc(w_fixed, 1)

            dve.wait_ge(experts_loaded, 16)
            dve.wait_ge(high_done, BATCH)
            fetch(0, 0)
            keep_gates(last - 1)
            normalize_h1(last)
            score_shifts(last)
            fetch(1, 1)
            pool_group(last)
            gate_logits(last)
            gate_top(last)
            keep_gates(last)
            fetch(2, 2)
            fetch(3, 3)

            def combine(b, u):
                dve.wait_ge(eo_ready, u + 1)
                dve.scalar_tensor_tensor(out=acc, in0=eo[0], scalar=gate_all[:, bass.ds(u, 1)],
                                         in1=rcols(h1, b), op0=ALU.mult, op1=ALU.add).then_inc(acc_ready, 1)

            def combine_last(b, u):
                dve.wait_ge(acc_ready, u)
                dve.wait_ge(eo_ready, u + 1)
                dve.scalar_tensor_tensor(out=rcols(out_sb, b), in0=eo[1], scalar=gate_all[:, bass.ds(u, 1)],
                                         in1=acc, op0=ALU.mult, op1=ALU.add).then_inc(acc_ready, 1)
                dve.wait_ge(acc_ready, u + 1)

            dve.wait_ge(gates_ready, 2 * GROUPS)
            with dve.Fori(0, UNITS // 4 - 1) as i:
                for n in range(2):
                    u = i * 4 + 2 * n
                    combine(i * 2 + n, u)
                    fetch(u + 4, 2 * n)
                    combine_last(i * 2 + n, u + 1)
                    fetch(u + 5, 2 * n + 1)
            for n in range(2):
                combine(BATCH - 2 + n, UNITS - 4 + 2 * n)
                combine_last(BATCH - 2 + n, UNITS - 3 + 2 * n)

        @block.tensor
        def _(pe):
            def mm(*args, **kw):
                return nc.tensor.matmul(*args, **kw)

            qkv = P("qkv")
            center = P("center")
            mean = P("ones_mean")

            def center_set(s):
                mm(set_bank(s, 0), center, set_view(h, s), start=True, stop=True).then_inc(ln1_centered[s], 1)

            def variance_set(s):
                pe.wait_ge(ln1_squared[s], 1)
                mm(set_bank(s, 1), mean, dense(sq1, s), start=True, stop=True).then_inc(ln1_var_done[s], 1)

            def project_set(s):
                pe.wait_ge(ln1_normed[s], 1)
                mm(set_bank(s, 2), qkv[:, 0:D], set_view(xn, s), start=True, stop=True).then_inc(q_done[s], 1)
                mm(set_bank(s, 3), qkv[:, D:2 * D], set_view(xn, s), start=True, stop=True).then_inc(k_done[s], 1)

            pe.wait_ge(patch_w_loaded, 16)
            for c in range(PATCH_CHUNKS):
                if c % 2 == 0:
                    pe.wait_ge(patches_loaded[c // 2], 16)
                last = mm(bank(0, TOK_COLS), patch_w[:, c, :], patch_in[:, c, :], start=(c == 0),
                          stop=(c == PATCH_CHUNKS - 1))
            last.then_inc(embed_done, 1)
            pe.wait_ge(params_loaded, 16)
            pe.wait_ge(text_a_loaded, 16)
            center_set(TEXT_A)
            pe.wait_ge(x_ready, 1)
            mm(bank(1, TOK_COLS), P("coord_spinor"), x_tok[:], start=True, stop=True).then_inc(coords_done, 1)
            pe.wait_ge(text_b_loaded, 16)
            center_set(TEXT_B)
            variance_set(TEXT_A)
            pe.wait_ge(setup_vec, 4)
            pe.wait_ge(coord_spin_ready, 2)
            mm(bank(2, TOK_COLS), P("embed"), coord_spin[:], start=True, stop=True)
            mm(bank(3, TOK_COLS), P("spinor_sum"), coord_spin[:], start=True, stop=True)
            mm(bank(3, 1, at=TOK_COLS), mean, P("b_attn_out"), start=True, stop=True).then_inc(manifold_done, 1)
            variance_set(TEXT_B)
            pe.wait_ge(enh_ready, 1)
            mm(bank(0, TOK_COLS), center, x_enh, start=True, stop=True).then_inc(tok_centered, 1)
            project_set(TEXT_A)
            pe.wait_ge(tok_squared, 1)
            mm(bank(1, TOK_COLS), mean, tok_sq, start=True, stop=True).then_inc(tok_var_done, 1)
            project_set(TEXT_B)
            pe.wait_ge(tok_normed, 1)
            mm(bank(2, TOK_COLS), P("tok_out"), tok_n, start=True, stop=True).then_inc(tok_out_done, 1)
            pe.wait_ge(w_out_step, 5)
            pe.wait_ge(tok_in_h, 1)
            center_set(IMG)
            variance_set(IMG)
            project_set(IMG)

            def denominators(g):
                pe.wait_ge(qk_sum_ready, g + 1)
                if g >= 2:
                    pe.wait_ge(den_log_ready, g - 1)
                mm(bank(POST_X + g % 2), P("block_ones"), gcols(qk_sum, g), start=True, stop=True)\
                    .then_inc(den_done, 1)

            def values(b):
                if b >= 1:
                    pe.wait_ge(v_ready, 2 * b)
                at = b * SEQ
                mm(bank(VALUE, D), xn[:, at:at + LO], qkv[:, 2 * D:3 * D], start=True, stop=True)
                mm(bank(VALUE, D, slice(0, HI), at=D), xn[:, at + LO:at + SEQ], qkv[:, 2 * D:3 * D], start=True,
                   stop=True).then_inc(v_done, 1)

            def scores_lo(b, n):
                at = b * SEQ
                if b % 4 == 0:
                    pe.wait_ge(q_heads_loaded[b // 4 * 2 + n], 64)
                if b >= 1:
                    pe.wait_ge(lo_masked, 2 * b - 1 + n)
                mm(bank(LO_A + n, 4 * LO), k_dec[:, at:at + LO], q_heads[:, 4 * n:4 * n + 4, at:at + LO],
                   start=True, stop=True).then_inc(lo_done, 1)

            def scores_tail(b):
                at = b * SEQ
                if b >= 1:
                    pe.wait_ge(tail_copied, b)
                mm(bank(TAIL, HEADS * HI), k_dec[:, at:at + LO], q_heads[:, :, at + LO:at + SEQ],
                   start=True, stop=True).then_inc(tail_done, 1)

            def scores_high(b):
                at = b * SEQ
                if b >= 1:
                    pe.wait_ge(high_masked, b)
                mm(bank(HIGH, HEADS * HI, slice(0, HI)), k_dec[:, at + LO:at + SEQ], q_heads[:, :, at + LO:at + SEQ],
                   start=True, stop=True).then_inc(high_done, 1)

            def attend(b):
                pe.wait_ge(v_ready, 2 * b + 2)
                pe.wait_ge(lo_masked, 2 * b + 2)
                pe.wait_ge(tail_copied, b + 1)
                pe.wait_ge(high_masked, b + 1)
                if b >= 1:
                    pe.wait_ge(att_ready, b)
                p = b % 2
                for r in range(2):
                    for vals, scs, rows, at in ((v_lo[p], s_lo[p], 128, 0), (v_hi[p], s_hi[p], HI, LO)):
                        for j in range(HEADS // 2):
                            last = mm(bank(AV, SEQ - at, slice(32 * j, 32 * j + 32), at=at),
                                      vals[0:rows, 2 * j + r, :], scs[0:rows, 2 * j + r, :],
                                      start=(r == 0 and at == 0), stop=(r == 1 and at > 0))
                last.then_inc(av_done, 1)

            def project_out(g):
                pe.wait_ge(att_ready, PER * (g + 1))
                if g == 0:
                    pe.wait_ge(den_log_ready, 3)
                elif g < GROUPS - 1:
                    pe.wait_ge(pool_exp_ready, PER * g)
                mm(bank(post_x(g)), w_out_c[:], gcols(att, g), start=True, stop=True).then_inc(out_done, 1)

            def variance_out(g):
                pe.wait_ge(out_squared, g + 1)
                if g == 0:
                    pe.wait_ge(den_log_ready, 4)
                elif g == 2:
                    pe.wait_ge(gates_ready, 2 * (g - 1))
                mm(bank(post_y(g)), mean, sq2[:, g % 2, :], start=True, stop=True).then_inc(out_var_done, 1)

            def center_h1(g):
                pe.wait_ge(h1_ready, g + 1)
                mm(bank(post_x(g)), center, gcols(h1, g), start=True, stop=True).then_inc(h1_centered, 1)

            def variance_h1(g):
                pe.wait_ge(h1_squared, g + 1)
                if 1 <= g < GROUPS - 1:
                    pe.wait_ge(gate_logits_ready, g)
                mm(bank(post_y(g)), mean, sq2[:, g % 2, :], start=True, stop=True).then_inc(h1_var_done, 1)

            def pool_scores(g):
                pe.wait_ge(h1_normed, g + 1)
                mm(bank(post_x(g)), pool_w128[:], gcols(xn3, g), start=True, stop=True).then_inc(score_done, 1)

            def gates(g):
                pe.wait_ge(pooled_ready, g + 1)
                if g < GROUPS - 2:
                    pe.wait_ge(out_log, g + 2)
                elif g == GROUPS - 2:
                    pe.wait_ge(gates_ready, 2 * g)
                mm(bank(post_y(g), EXPERTS, slice(0, PER)), pooled[:, PER * g:PER * g + PER], P("gate"),
                   start=True, stop=True).then_inc(gate_done, 1)

            def spread_gates(g):
                pe.wait_ge(gate_rows_ready, 2 * (g + 1))
                if g < GROUPS - 2:
                    pe.wait_ge(h1_log, g + 2)
                mm(bank(post_y(g), 2 * PER * TOP), ones[0:PER, 0:128], gate_rows[:, g, :, :].rearrange("p k n -> p (k n)"),
                   start=True, stop=True).then_inc(gate_bcast_done, 1)

            denominators(0)
            denominators(1)
            for b in range(BATCH):
                g = b // 2
                values(b)
                scores_lo(b, 0)
                if b % 2 == 1 and g >= 1:
                    project_out(g - 1)
                scores_lo(b, 1)
                if b % 2 == 1 and g >= 1:
                    variance_out(g - 1)
                if b % 2 == 0 and g >= 2:
                    variance_h1(g - 2)
                scores_tail(b)
                scores_high(b)
                if b >= 1:
                    attend(b - 1)
                if b == 0:
                    denominators(2)
                    denominators(3)
                if b % 2 == 0:
                    if g >= 2:
                        pool_scores(g - 2)
                    if g >= 3:
                        spread_gates(g - 3)
                else:
                    if g >= 2:
                        gates(g - 2)
                    if g >= 1:
                        center_h1(g - 1)
            last = GROUPS - 1
            attend(BATCH - 1)
            variance_h1(last - 1)
            project_out(last)
            pool_scores(last - 1)
            spread_gates(last - 2)
            variance_out(last)
            center_h1(last)
            gates(last - 1)
            variance_h1(last)
            spread_gates(last - 1)

            def up(u, k, b):
                pe.wait_ge(w_fixed, u + 1)
                if not isinstance(u, int) or u >= 2:
                    pe.wait_ge(hid_ready, u * 4 - 4)
                for c in range(HID_CHUNKS):
                    last = mm(bank(2 * (k % 2) + c // 2, SEQ, at=(c % 2) * SEQ),
                              w_fix[k][:, W1_AT + 128 * c:W1_AT + 128 * (c + 1)], rcols(xn3, b), start=True, stop=True)
                    if c % 2:
                        last.then_inc(up_done, 1)

            def down(u, k):
                pe.wait_ge(hid_ready, u * 4 + 4)
                if not isinstance(u, int) or u >= 2:
                    pe.wait_ge(eo_ready, u - 1)
                for c in range(HID_CHUNKS):
                    last = mm(bank(4 + k % 2, SEQ), w_fix[k][:, W2_AT + 128 * c:W2_AT + 128 * (c + 1)],
                              hid[k % 2][:, c, :], start=(c == 0), stop=(c == HID_CHUNKS - 1))
                last.then_inc(down_done, 1)

            up(0, 0, 0)
            pool_scores(last)
            up(1, 1, 0)
            gates(last)
            spread_gates(last)
            pe.wait_ge(gates_ready, 2 * GROUPS)
            down(0, 0)
            for k in (2, 3):
                up(k, k, k // TOP)
                down(k - 1, k - 1)
            with pe.Fori(1, UNITS // 4) as i:
                for k in range(4):
                    up(i * 4 + k, k, i * 2 + k // 2)
                    down(i * 4 + (k - 1), (k + 3) % 4)
            down(UNITS - 1, 3)


def _param_array(t):
    prm = np.zeros((128, PARAM_COLS), np.float32)

    def put(name, a, row=0):
        at, n = AT[name]
        a = np.asarray(a, np.float32)
        a = a[:, None] if a.ndim == 1 else a
        prm[row:row + a.shape[0], at:at + a.shape[1]] = a

    at, _ = AT["coord_spinor"]
    put("coord_spinor", t["L0_tok_W_coord"])
    prm[:, at + SPINOR_AT:at + SPINOR_AT + SPINOR] = t["L0_tok_W_spinor"]
    put("embed", t["L0_tok_W_embed"])
    put("tok_out", t["L0_tok_W_out"])
    put("qkv", t["L0_attn_W_qkv"])
    put("attn_out", t["L0_attn_W_out"])
    put("gate", t["L0_ffn_gate_w"])
    put("bias_v", np.broadcast_to(t["L0_attn_b_qkv"][2 * D:], (128, D)))
    put("bias_gate", np.broadcast_to(t["L0_ffn_gate_b"], (128, EXPERTS)))
    put("pos", t["L0_tok_pos_embed"][0].T)
    put("ones_mean", np.full((128, D), 1.0 / D))
    put("center", np.eye(D) - 1.0 / D)
    put("spinor_sum", np.ones((SPINOR, D)), SPINOR_AT)
    head_of = np.arange(D) // HEAD
    put("block_ones", head_of[:, None] == head_of[None, :])
    put("causal", np.arange(LO)[None, :] >= np.arange(128)[:, None])
    put("position", np.broadcast_to(np.arange(SEQ), (128, SEQ)))
    put("diag", np.repeat(np.eye(BATCH), TOP, axis=1))
    put("b_patch", t["L0_tok_b_patch"])
    put("b_coord_spinor", t["L0_tok_b_coord"])
    put("b_coord_spinor", t["L0_tok_b_spinor"], SPINOR_AT)
    put("b_embed", t["L0_tok_b_embed"])
    put("tok_gamma", t["L0_tok_ln_gamma"])
    put("tok_beta", t["L0_tok_ln_beta"])
    put("b_tok_out", t["L0_tok_b_out"])
    put("b_q", t["L0_attn_b_qkv"][:D])
    put("b_k", t["L0_attn_b_qkv"][D:2 * D])
    put("b_attn_out", t["L0_attn_b_out"])
    put("decay", np.repeat(t["L0_attn_decay_logits"], HEAD))
    put("attn_gamma", t["L0_attn_ln_g"])
    put("attn_beta", t["L0_attn_ln_b"])
    put("pool_w", t["L0_ffn_attn_w"])
    put("pool_b", np.broadcast_to(t["L0_ffn_attn_b"], (128,)))
    return prm


def kernel(**inputs):
    import concourse.bacc as _bacc
    from concourse.bass_utils import run_bass_kernel_spmd as _run

    t = {k: np.asarray(v) for k, v in inputs.items()}
    patches = t["x"].reshape(BATCH, CHANNELS, GRID, PATCH, GRID, PATCH).transpose(1, 3, 5, 0, 2, 4)
    arrays = {
        "patches": patches.reshape(PATCH_CHUNKS, 128, TOK_COLS).transpose(1, 0, 2),
        "text": t["txt"].transpose(2, 0, 1),
        "w_patch": t["L0_tok_W_patch"].reshape(PATCH_CHUNKS, 128, D).transpose(1, 0, 2),
        "params": _param_array(t),
        "experts": np.concatenate([
            t["L0_ffn_w1"].transpose(1, 0, 2),
            t["L0_ffn_w2"].reshape(EXPERTS, HID_CHUNKS, 128, D).transpose(2, 0, 1, 3).reshape(128, EXPERTS, HIDDEN),
            t["L0_ffn_b1"].reshape(EXPERTS, HID_CHUNKS, 128).transpose(2, 0, 1),
            t["L0_ffn_b2"].T[:, :, None]], axis=2),
    }
    nc = _bacc.Bacc("TRN2", target_bir_lowering=False, num_devices=1)
    arrays = {k: np.ascontiguousarray(a) for k, a in arrays.items()}
    args = [nc.dram_tensor(k, a.shape, mybir.dt.from_np(a.dtype), kind="ExternalInput").ap()
            for k, a in arrays.items()]
    out = nc.dram_tensor("out", (D, COLS), F32, kind="ExternalOutput").ap()
    build(nc, *args, out)
    r = _run(nc, [arrays], core_ids=[0])
    return np.ascontiguousarray(r.results[0]["out"].reshape(D, BATCH, SEQ).transpose(1, 2, 0))
```

```python
from contextlib import ExitStack

import numpy as np

import concourse.bass as bass
from concourse import mybir

F32 = mybir.dt.float32
I32 = mybir.dt.int32
U32 = mybir.dt.uint32
ALU = mybir.AluOpType
ACT = mybir.ActivationFunctionType
AX_X = mybir.AxisListType.X

BATCH, CHANNELS, IMAGE, PATCH = 8, 3, 112, 16
GRID = IMAGE // PATCH
PATCHES = GRID * GRID
PATCH_DIM = CHANNELS * PATCH * PATCH
PATCH_CHUNKS = PATCH_DIM // 128
TEXT = 128
D = 128
COORDS, SPINOR = 8, 4
SPINOR_AT = 32
SEQ = PATCHES + TEXT
COLS = BATCH * SEQ
TOK_COLS = BATCH * PATCHES
TOK_HALF = TOK_COLS // 2
HEADS = 8
HEAD = D // HEADS
EXPERTS, HIDDEN, TOP = 8, 512, 2
HID_CHUNKS = HIDDEN // 128
EPS = 1e-5

PER = 2
GROUPS = BATCH // PER
GC = PER * SEQ
BANK = 512
LO = 128
HI = SEQ - LO
UNITS = BATCH * TOP
WARM_UPS = 10
LATE_GROUPS = (GROUPS - 2, GROUPS - 1)

TEXT_A, TEXT_B, IMG_A, IMG_B = range(4)
SET_COLS = (BATCH // 2 * TEXT, BATCH // 2 * TEXT, TOK_HALF, TOK_HALF)
SET_AT = [sum(SET_COLS[:n]) for n in range(5)]

MATS = [("center", D), ("ones_mean", D), ("coord_spinor", D), ("pos", PATCHES), ("embed", D), ("spinor_sum", D), ("tok_out", D), ("qkv", 3 * D), ("attn_out", D), ("gate", EXPERTS),
        ("bias_v", D), ("bias_gate", EXPERTS),
         ("block_ones", D), ("causal", LO), ("causal_hi", HI), ("position", SEQ),
        ("diag", BATCH * TOP), ("head_mask", HEADS)]
VECS = ["b_patch", "b_coord_spinor", "b_embed", "tok_gamma", "tok_beta", "b_tok_out", "b_q", "b_k", "b_attn_out",
        "decay", "attn_gamma", "attn_beta", "pool_w", "pool_b"]
EARLY = 6
AT = {}
for _name, _n in MATS[:EARLY] + [(_v, 1) for _v in VECS] + MATS[EARLY:]:
    AT[_name] = (sum(n for _, n in AT.values()), _n)
PARAM_COLS = sum(n for _, n in AT.values())
EARLY_COLS = AT[MATS[EARLY][0]][0]
W1_AT, W2_AT, B1_AT, B2_AT = 0, HIDDEN, 2 * HIDDEN, 2 * HIDDEN + HID_CHUNKS
EXPERT_COLS = B2_AT + 1


def build(nc, patches, text, w_patch, params, experts, out):
    ctx = ExitStack()
    with ctx:
        def sb(name, shape, dt=F32):
            return ctx.enter_context(nc.sbuf_tensor(name, shape, dt))

        def sem(name):
            return ctx.enter_context(nc.semaphore(name))

        prm = sb("prm", [128, PARAM_COLS])
        patch_in = sb("patch_in", [128, 2, PATCH_CHUNKS, TOK_HALF])
        patch_w = sb("patch_w", [128, PATCH_CHUNKS, D])
        expert_w = sb("expert_w", [128, EXPERTS, EXPERT_COLS])
        x_tok = sb("x_tok", [128, 2, TOK_HALF])
        coord_spin = sb("coord_spin", [128, 2, TOK_HALF])
        manifold, x_enh, tok_sq, tok_log, tok_rstd, tok_n = [patch_in[:, :, n, :] for n in range(PATCH_CHUNKS)]
        h = sb("h", [128, COLS])
        h_beta = sb("h_beta", [128, COLS])
        xn = sb("xn", [128, COLS])
        q_dec = sb("q_dec", [128, COLS])
        k_dec = sb("k_dec", [128, COLS])
        k_sum = sb("k_sum", [128, COLS])
        qk_sum = sb("qk_sum", [128, COLS])
        den_log = k_sum
        rden = sb("rden", [128, COLS])
        att = sb("att", [128, COLS])
        sq1 = sb("sq1", [128, SET_AT[-1]])
        rstd1 = sb("rstd1", [128, SET_AT[-1]])
        q_exp = sb("q_exp", [128, SET_AT[-1]])
        q_pos = sb("q_pos", [128, SET_AT[-1]])
        k_exp = sb("k_exp", [128, SET_AT[-1]])
        k_pos = sb("k_pos", [128, SET_AT[-1]])
        q_heads = sb("q_heads", [128, HEADS, COLS])
        decay_heads = sb("decay_heads", [128, HEADS, PATCHES])
        decay_q = sb("decay_q", [128, SEQ])
        decay_k = sb("decay_k", [128, SEQ])
        ones = sb("ones", [128, SEQ])
        lam = sb("lam", [128, 8])
        w_out_c = sb("w_out_c", [128, D])
        out_stat = sb("out_stat", [128, 4])
        pool_w128 = sb("pool_w128", [128, 128])
        eps_col = sb("eps_col", [128, 2])
        euler = sb("euler", [PER, EXPERTS])
        v_lo = [sb(f"v_lo{p}", [128, HEADS, 2 * HEAD]) for p in range(2)]
        v_hi = [sb(f"v_hi{p}", [128, HEADS // 2, 2 * HEAD]) for p in range(2)]
        s_lo = [sb(f"s_lo{p}", [128, HEADS, SEQ]) for p in range(2)]
        s_hi = [sb(f"s_hi{p}", [128, HEADS // 2, HI]) for p in range(2)]
        sq2 = sq1[:, 0:2 * GC].rearrange("p (n c) -> p n c", n=2)
        rstd2 = rstd1[:, 0:2 * GC].rearrange("p (n c) -> p n c", n=2)
        attn_x = q_exp[:, 0:2 * GC].rearrange("p (n c) -> p n c", n=2)
        h1 = q_dec
        xn3 = k_sum
        pool_exp = qk_sum
        pool_prod = k_dec
        score_neg_max = sb("score_neg_max", [128, BATCH])
        score_bias = sb("score_bias", [128, BATCH])
        exp_sum = sb("exp_sum", [128, BATCH])
        exp_rsum = sb("exp_rsum", [128, BATCH])
        pooled_raw = sb("pooled_raw", [128, BATCH])
        pooled = sb("pooled", [128, BATCH])
        gl = sb("gl", [PER, GROUPS, 5, EXPERTS])
        gate_idx = sb("gate_idx", [PER, GROUPS, EXPERTS], U32)
        gate_cat = sb("gate_cat", [PER, GROUPS, 2, TOP])
        gate_rows = sb("gate_rows", [PER, GROUPS, 2, PER * TOP])
        gate_all = sb("gate_all", [128, UNITS])
        expert_of = sb("expert_of", [1, UNITS], I32)
        w_fix = [q_heads[:, k, 0:EXPERT_COLS] for k in range(4)]
        hid = [q_heads[:, 4 + k, 0:HID_CHUNKS * SEQ].rearrange("p (c l) -> p c l", c=HID_CHUNKS) for k in range(2)]
        eo = [q_heads[:, 6, k * SEQ:(k + 1) * SEQ] for k in range(2)]
        acc = q_heads[:, 7, 0:SEQ]
        out_sb = rden
        ps = ctx.enter_context(nc.psum_tensor("ps", [128, 8 * BANK], F32))

        def P(name):
            at, n = AT[name]
            return prm[:, at:at + n]

        def bank(k, n=GC, rows=slice(0, 128), at=0):
            return ps[rows, k * BANK + at:k * BANK + at + n]

        def hi_rows(n):
            return slice(64 * n, 64 * n + HI)

        def gcols(t, g):
            return t[:, g * GC:(g + 1) * GC]

        def bcols(t, b):
            return t[:, b * SEQ:(b + 1) * SEQ]

        def rcols(t, b):
            return t[:, bass.ds(b * SEQ, SEQ)]

        LO_A, LO_B, TAIL, HIGH, VALUE, AV, POST_X, POST_Y = range(8)

        def post_x(g):
            return VALUE if g == GROUPS - 1 else POST_X

        def post_y(g):
            return AV if g == GROUPS - 1 else POST_Y

        SET_BANKS = ((4, 5, 5, 4), (6, 7, 7, 6), (1, 0, 0, 1), (3, 2, 2, 3))

        def set_view(t, s):
            half = s % 2
            by_batch = t[:, :].rearrange("p (b l) -> p b l", b=BATCH)[:, half * BATCH // 2:(half + 1) * BATCH // 2, :]
            return by_batch[:, :, 0:PATCHES] if s >= IMG_A else by_batch[:, :, PATCHES:SEQ]

        def shaped(flat):
            return flat.rearrange("p (b l) -> p b l", b=BATCH // 2)

        def set_bank(s, which):
            return bank(SET_BANKS[s][which], SET_COLS[s])

        def dense(t, s):
            return t[:, SET_AT[s]:SET_AT[s + 1]]

        def set_decay(t, s):
            part = t[:, 0:PATCHES] if s >= IMG_A else t[:, PATCHES:SEQ]
            return part.unsqueeze(1).to_broadcast([128, BATCH // 2, part.shape[1]])

        def tok_bank(a, which):
            return bank(2 * a + which, TOK_HALF)

        patch_w_loaded = sem("patch_w_loaded")
        early_params_loaded = sem("early_params_loaded")
        patches_loaded = [sem(f"patches_loaded{n}") for n in range(2)]
        params_loaded = sem("params_loaded")
        q_heads_zeroed = sem("q_heads_zeroed")
        q_dec_ready = [sem(f"q_dec_ready{n}") for n in range(4)]
        q_heads_loaded = [sem(f"q_heads_loaded{n}") for n in range(4)]
        experts_loaded = sem("experts_loaded")
        acc_ready = sem("acc_ready")
        out_stored = sem("out_stored")
        q_elu_ready = [sem(f"q_elu_ready{n}") for n in range(4)]
        k_elu_ready = [sem(f"k_elu_ready{n}") for n in range(4)]
        k_dec_ready = [sem(f"k_dec_ready{n}") for n in range(4)]
        k_sum_ready = sem("k_sum_ready")
        qk_sum_ready = sem("qk_sum_ready")
        decay_ready = sem("decay_ready")
        gates_shifted = sem("gates_shifted")
        gate_exp_ready = sem("gate_exp_ready")
        text_loaded = [sem(f"text_loaded{n}") for n in range(2)]
        setup_act = sem("setup_act")
        ln1_centered = [sem(f"ln1_centered{n}") for n in range(4)]
        ln1_squared = [sem(f"ln1_squared{n}") for n in range(4)]
        ln1_var_done = [sem(f"ln1_var_done{n}") for n in range(4)]
        ln1_log = [sem(f"ln1_log{n}") for n in range(4)]
        ln1_rstd_ready = [sem(f"ln1_rstd_ready{n}") for n in range(4)]
        q_done = [sem(f"q_done{n}") for n in range(4)]
        q_parts_ready = [sem(f"q_parts_ready{n}") for n in range(4)]
        k_done = [sem(f"k_done{n}") for n in range(4)]
        k_parts_ready = [sem(f"k_parts_ready{n}") for n in range(4)]
        setup_vec = sem("setup_vec")
        coords_done = sem("coords_done")
        spinor_ready = sem("spinor_ready")
        manifold_done = sem("manifold_done")
        manifold_ready = sem("manifold_ready")
        tok_centered = sem("tok_centered")
        tok_squared = sem("tok_squared")
        tok_var_done = sem("tok_var_done")
        tok_log_ready = sem("tok_log_ready")
        tok_rstd_ready = sem("tok_rstd_ready")
        den_done = sem("den_done")
        den_log_ready = sem("den_log_ready")
        rden_ready = sem("rden_ready")
        tail_done = sem("tail_done")
        av_done = sem("av_done")
        tail_copied = sem("tail_copied")
        out_done = sem("out_done")
        out_squared = sem("out_squared")
        out_var_done = sem("out_var_done")
        out_log = sem("out_log")
        out_rstd_ready = sem("out_rstd_ready")
        h1_centered = sem("h1_centered")
        h1_squared = sem("h1_squared")
        h1_var_done = sem("h1_var_done")
        h1_log = sem("h1_log")
        h1_rstd_ready = sem("h1_rstd_ready")
        score_bias_ready = sem("score_bias_ready")
        pool_exp_ready = sem("pool_exp_ready")
        down_done = sem("down_done")
        up_done = sem("up_done")
        hid_ready = sem("hid_ready")
        gate_shift_ready = sem("gate_shift_ready")
        eo_ready = sem("eo_ready")
        v_zeroed = sem("v_zeroed")
        w_out_step = sem("w_out_step")
        v_done = sem("v_done")
        embed_done = sem("embed_done")
        x_ready = sem("x_ready")
        coords_ready = sem("coords_ready")
        enh_mul = sem("enh_mul")
        enh_ready = sem("enh_ready")
        tok_mul = sem("tok_mul")
        tok_normed = sem("tok_normed")
        tok_out_done = sem("tok_out_done")
        tok_in_h = sem("tok_in_h")
        ln1_normed = [sem(f"ln1_normed{n}") for n in range(4)]
        q_heads_spread = [sem(f"q_heads_spread{n}") for n in range(2)]
        k_pos_ready = [sem(f"k_pos_ready{n}") for n in range(4)]
        h_beta_ready = sem("h_beta_ready")
        v_ready = sem("v_ready")
        lo_done = sem("lo_done")
        lo_masked = sem("lo_masked")
        high_done = sem("high_done")
        high_masked = sem("high_masked")
        att_ready = sem("att_ready")
        h1_ready = sem("h1_ready")
        out_mul = sem("out_mul")
        h1_normed = sem("h1_normed")
        score_done = sem("score_done")
        score_max_ready = sem("score_max_ready")
        pooled_step = sem("pooled_step")
        pooled_ready = sem("pooled_ready")
        gate_done = sem("gate_done")
        gate_logits_ready = sem("gate_logits_ready")
        gate_step = sem("gate_step")
        gate_rows_ready = sem("gate_rows_ready")
        gates_summed = sem("gates_summed")
        gate_bcast_done = sem("gate_bcast_done")
        gates_ready = sem("gates_ready")
        w_fixed = sem("w_fixed")

        block = ctx.enter_context(nc.Block())

        @block.sync
        def _(sp):
            sp.dma_start(patch_w[:], w_patch).then_inc(patch_w_loaded, 16)
            sp.dma_start(prm[:, 0:EARLY_COLS], params[:, 0:EARLY_COLS]).then_inc(early_params_loaded, 16)
            sp.dma_start(patch_in[:, 1, :, :], patches[:, 1, :, :]).then_inc(patches_loaded[1], 16)
            sp.dma_start(prm[:, EARLY_COLS:PARAM_COLS], params[:, EARLY_COLS:PARAM_COLS]).then_inc(params_loaded, 16)
            sp.wait_ge(q_heads_zeroed, 1)
            for s in (TEXT_A, TEXT_B):
                sp.wait_ge(q_dec_ready[s], 1)
                for hd in range(HEADS):
                    rows = slice(HEAD * hd, HEAD * hd + HEAD)
                    sp.dma_start(set_view(q_heads[:, hd, :], s)[rows], set_view(q_dec, s)[rows])\
                        .then_inc(q_heads_loaded[2 * s + hd // 4], 16)
                if s == TEXT_A:
                    sp.dma_start(expert_w[:], experts).then_inc(experts_loaded, 16)
            with sp.Fori(0, BATCH) as b:
                at = sp.snap(b * SEQ)
                added = sp.snap(b * TOP + TOP)
                sp.wait_ge(acc_ready, added)
                sp.dma_start(out[:, bass.ds(at, SEQ)], out_sb[:, bass.ds(at, SEQ)]).then_inc(out_stored, 16)
            sp.wait_ge(out_stored, 16 * BATCH)

        @block.gpsimd
        def _(pool):
            nc.gpsimd.memset(q_heads[:, :, :].rearrange("p h (b l) -> p (h b) l", l=SEQ)[:, :, PATCHES:SEQ], 0.0)\
                .then_inc(q_heads_zeroed, 1)

            def decay(s, what):
                if what == "q":
                    pool.wait_ge(q_elu_ready[s], 1)
                    nc.gpsimd.tensor_tensor(set_view(q_dec, s), shaped(dense(q_pos, s)), set_decay(decay_q, s),
                                            ALU.mult).then_inc(q_dec_ready[s], 1)
                else:
                    pool.wait_ge(k_elu_ready[s], 1)
                    nc.gpsimd.tensor_tensor(set_view(k_dec, s), shaped(dense(k_pos, s)), set_decay(decay_k, s),
                                            ALU.mult).then_inc(k_dec_ready[s], 1)

            def multiply_sums(g):
                pool.wait_ge(q_dec_ready[TEXT_A + g // 2], 1)
                pool.wait_ge(q_dec_ready[IMG_A + g // 2], 1)
                pool.wait_ge(k_sum_ready, PER * (g + 1))
                nc.gpsimd.tensor_tensor(gcols(qk_sum, g), gcols(q_dec, g), gcols(k_sum, g),
                                        ALU.mult).then_inc(qk_sum_ready, 1)

            pool.wait_ge(decay_ready, 3)
            for s, what in ((TEXT_A, "k"), (IMG_A, "k"), (IMG_A, "q")):
                decay(s, what)
            multiply_sums(0)
            multiply_sums(1)
            decay(TEXT_B, "q")
            decay(TEXT_B, "k")
            decay(IMG_B, "q")
            multiply_sums(2)
            multiply_sums(3)
            for g in LATE_GROUPS:
                pool.wait_ge(gates_shifted, g - LATE_GROUPS[0] + 1)
                nc.gpsimd.tensor_tensor(gl[:, g, 2, :], euler[:], gl[:, g, 4, :], ALU.pow).then_inc(gate_exp_ready, 1)

        @block.scalar
        def _(act):
            nc.scalar.dma_start(patch_in[:, 0, :, :], patches[:, 0, :, :]).then_inc(patches_loaded[0], 16)
            nc.scalar.dma_start(set_view(h, TEXT_A), text[:, 0:BATCH // 2, :]).then_inc(text_loaded[0], 16)
            nc.scalar.dma_start(set_view(h, TEXT_B), text[:, BATCH // 2:BATCH, :]).then_inc(text_loaded[1], 16)
            nc.scalar.preload_act_table_set("natural_log_exp_and_others")
            act.wait_ge(early_params_loaded, 16)
            nc.scalar.activation(lam[:, 0:1], P("decay"), ACT.Exp, scale=-1.0).then_inc(setup_act, 1)

            def square_of_set(s):
                act.wait_ge(ln1_centered[s], 1)
                nc.scalar.activation(dense(sq1, s), set_bank(s, 0), ACT.Square).then_inc(ln1_squared[s], 1)

            def rstd_of_set(s):
                act.wait_ge(ln1_var_done[s], 1)
                nc.scalar.activation(dense(sq1, s), set_bank(s, 1), ACT.Ln, bias=eps_col[:, 0:1])\
                    .then_inc(ln1_log[s], 1)
                act.wait_ge(ln1_log[s], 1)
                nc.scalar.activation(dense(rstd1, s), dense(sq1, s), ACT.Exp, scale=-0.5)\
                    .then_inc(ln1_rstd_ready[s], 1)

            def q_parts(s):
                act.wait_ge(q_done[s], 1)
                nc.scalar.activation(dense(q_exp, s), set_bank(s, 2), ACT.Exp, bias=P("b_q"))\
                    .then_inc(q_parts_ready[s], 1)
                nc.scalar.activation(dense(q_pos, s), set_bank(s, 2), ACT.Relu, bias=P("b_q"))\
                    .then_inc(q_parts_ready[s], 1)

            def k_parts(s):
                act.wait_ge(k_done[s], 1)
                nc.scalar.activation(dense(k_exp, s), set_bank(s, 3), ACT.Exp, bias=P("b_k"))\
                    .then_inc(k_parts_ready[s], 1)
                if s in (TEXT_B, IMG_B):
                    nc.scalar.activation(dense(k_pos, s), set_bank(s, 3), ACT.Relu, bias=P("b_k"))\
                        .then_inc(k_parts_ready[s], 1)

            def decays():
                act.wait_ge(setup_vec, 7)
                nc.scalar.activation(lam[:, 4:5], lam[:, 3:4], ACT.Ln).then_inc(setup_act, 1)
                act.wait_ge(setup_act, 2)
                nc.scalar.mul(lam[:, 5:6], lam[:, 4:5], -1.0).then_inc(setup_act, 1)
                act.wait_ge(setup_act, 3)
                act.wait_ge(params_loaded, 16)
                nc.scalar.activation(decay_q[:], P("position"), ACT.Exp, scale=lam[:, 4:5]).then_inc(decay_ready, 1)
                nc.scalar.activation(decay_k[:], P("position"), ACT.Exp, scale=lam[:, 5:6]).then_inc(decay_ready, 1)

            def spinor_square(a):
                rows = slice(SPINOR_AT, SPINOR_AT + SPINOR)
                act.wait_ge(coords_done, a + 1)
                act.wait_ge(setup_vec, 4)
                nc.scalar.activation(coord_spin[rows, a, :], bank(2 * a + 1, TOK_HALF, rows), ACT.Square,
                                     bias=P("b_coord_spinor")[rows, :]).then_inc(spinor_ready, 1)

            def manifold_bias(a):
                act.wait_ge(manifold_done, a + 1)
                nc.scalar.activation(manifold[:, a, :], tok_bank(a, 0), ACT.Identity, bias=P("b_embed"))\
                    .then_inc(manifold_ready, 1)

            def tok_square(a):
                act.wait_ge(tok_centered, a + 1)
                nc.scalar.activation(tok_sq[:, a, :], tok_bank(a, 0), ACT.Square).then_inc(tok_squared, 1)

            def tok_rstds(a):
                act.wait_ge(tok_var_done, a + 1)
                nc.scalar.activation(tok_log[:, a, :], tok_bank(a, 1), ACT.Ln, bias=eps_col[:, 0:1])\
                    .then_inc(tok_log_ready, 1)
                act.wait_ge(tok_log_ready, a + 1)
                nc.scalar.activation(tok_rstd[:, a, :], tok_log[:, a, :], ACT.Exp, scale=-0.5)\
                    .then_inc(tok_rstd_ready, 1)

            spinor_square(0)
            square_of_set(TEXT_A)
            decays()
            manifold_bias(0)
            rstd_of_set(TEXT_A)
            tok_square(0)
            spinor_square(1)
            tok_rstds(0)
            manifold_bias(1)
            q_parts(TEXT_A)
            tok_square(1)
            square_of_set(IMG_A)
            k_parts(TEXT_A)
            tok_rstds(1)
            rstd_of_set(IMG_A)
            square_of_set(TEXT_B)
            q_parts(IMG_A)
            k_parts(IMG_A)
            square_of_set(IMG_B)
            rstd_of_set(TEXT_B)
            rstd_of_set(IMG_B)
            q_parts(TEXT_B)
            q_parts(IMG_B)
            k_parts(IMG_B)
            k_parts(TEXT_B)
            def den_reciprocal(g):
                act.wait_ge(den_done, g + 1)
                nc.scalar.activation(gcols(den_log, g), bank(POST_X + g % 2), ACT.Ln, bias=eps_col[:, 1:2])\
                    .then_inc(den_log_ready, 1)
                act.wait_ge(den_log_ready, g + 1)
                nc.scalar.activation(gcols(rden, g), gcols(den_log, g), ACT.Exp, scale=-1.0)\
                    .then_inc(rden_ready, 1)

            def copy_tail(b):
                act.wait_ge(tail_done, b + 1)
                if b >= 2:
                    act.wait_ge(av_done, b - 1)
                nc.scalar.activation(s_lo[b % 2][:, :, LO:SEQ],
                                     bank(TAIL, HEADS * HI).rearrange("p (a l) -> p a l", a=HEADS),
                                     ACT.Copy).then_inc(tail_copied, 1)

            def square_out(g):
                act.wait_ge(out_done, g + 1)
                nc.scalar.activation(sq2[:, g % 2, :], bank(post_x(g)), ACT.Square, bias=out_stat[:, 3:4])\
                    .then_inc(out_squared, 1)

            def rstd_out(g):
                act.wait_ge(out_var_done, g + 1)
                nc.scalar.activation(sq2[:, g % 2, :], bank(post_y(g)), ACT.Ln, bias=eps_col[:, 0:1])\
                    .then_inc(out_log, 1)
                act.wait_ge(out_log, g + 1)
                nc.scalar.activation(rstd2[:, g % 2, :], sq2[:, g % 2, :], ACT.Exp, scale=-0.5)\
                    .then_inc(out_rstd_ready, 1)

            def square_h1(g):
                act.wait_ge(h1_centered, g + 1)
                nc.scalar.activation(sq2[:, g % 2, :], bank(post_x(g)), ACT.Square).then_inc(h1_squared, 1)

            def rstd_h1(g):
                act.wait_ge(h1_var_done, g + 1)
                nc.scalar.activation(sq2[:, g % 2, :], bank(post_y(g)), ACT.Ln, bias=eps_col[:, 0:1])\
                    .then_inc(h1_log, 1)
                act.wait_ge(h1_log, g + 1)
                nc.scalar.activation(rstd2[:, g % 2, :], sq2[:, g % 2, :], ACT.Exp, scale=-0.5)\
                    .then_inc(h1_rstd_ready, 1)

            def exp_pool(g):
                act.wait_ge(score_bias_ready, g + 1)
                for b in (PER * g, PER * g + 1):
                    nc.scalar.activation(bcols(pool_exp, b), bank(post_x(g), SEQ, at=(b % PER) * SEQ), ACT.Exp,
                                         bias=score_bias[:, b:b + 1], accum_out=exp_sum[:, b:b + 1])\
                        .then_inc(pool_exp_ready, 1)

            def gelu_hidden(u, k):
                if not isinstance(u, int) or u >= 2:
                    act.wait_ge(down_done, u - 1)
                for c in range(HID_CHUNKS):
                    if c % 2 == 0:
                        act.wait_ge(up_done, u * 2 + (c // 2 + 1))
                    nc.scalar.activation(hid[k % 2][:, c, :], bank(2 * (k % 2) + c // 2, SEQ, at=(c % 2) * SEQ),
                                         ACT.Gelu, bias=w_fix[k][:, B1_AT + c:B1_AT + c + 1]).then_inc(hid_ready, 1)

            def exp_gate(g):
                act.wait_ge(gate_shift_ready, g + 1)
                nc.scalar.activation(gl[:, g, 2, :], gl[:, g, 0, :], ACT.Exp, bias=gl[:, g, 1, 0:1],
                                     accum_out=gl[:, g, 1, 1:2]).then_inc(gate_exp_ready, 1)

            for b in range(BATCH):
                g = b // 2
                if b % 2 == 0:
                    if g >= 2:
                        square_h1(g - 2)
                        rstd_h1(g - 2)
                    copy_tail(b)
                    if g >= 2:
                        exp_pool(g - 2)
                else:
                    if g >= 1:
                        square_out(g - 1)
                        rstd_out(g - 1)
                    copy_tail(b)
                    if g >= 2:
                        exp_gate(g - 2)
                if b < 2:
                    den_reciprocal(b)
                elif b == 2:
                    den_reciprocal(2)
                    den_reciprocal(3)
            last = GROUPS - 1
            square_h1(last - 1)
            square_out(last)
            rstd_h1(last - 1)
            rstd_out(last)
            nc.scalar.preload_act_table(ACT.Gelu)
            gelu_hidden(0, 0)
            square_h1(last)
            nc.scalar.preload_act_table_set("natural_log_exp_and_others")
            rstd_h1(last)
            exp_pool(last - 1)
            exp_pool(last)
            nc.scalar.preload_act_table(ACT.Gelu)

            def gelu_out(u, k):
                act.wait_ge(down_done, u + 1)
                if not isinstance(u, int) or u >= 2:
                    act.wait_ge(acc_ready, u - 1)
                nc.scalar.activation(eo[k % 2], bank(4 + k % 2, SEQ), ACT.Gelu,
                                     bias=w_fix[k][:, B2_AT:B2_AT + 1]).then_inc(eo_ready, 1)

            for k in range(3):
                gelu_hidden(k + 1, k + 1)
                gelu_out(k, k)
            with act.Fori(1, UNITS // 4) as i:
                for k in range(4):
                    gelu_hidden(i * 4 + k, k)
                    gelu_out(i * 4 + (k - 1), (k + 3) % 4)
            gelu_out(UNITS - 1, 3)

        @block.vector
        def _(dve):
            dve.memset(eps_col[:, 0:1], EPS).then_inc(setup_vec, 1)
            dve.memset(eps_col[:, 1:2], 1e-6).then_inc(setup_vec, 1)
            dve.memset(ones[:], 1.0).then_inc(setup_vec, 1)
            dve.memset(coord_spin[:], 0.0).then_inc(setup_vec, 1)
            dve.memset(euler[:], float(np.e)).then_inc(v_zeroed, 1)
            for p in range(2):
                dve.memset(v_lo[p][:], 0.0).then_inc(v_zeroed, 1)
                dve.memset(v_hi[p][:], 0.0).then_inc(v_zeroed, 1)
            dve.wait_ge(setup_act, 1)
            dve.tensor_scalar(lam[:, 1:2], lam[:, 0:1], 1.0, None, ALU.add).then_inc(setup_vec, 1)
            dve.wait_ge(setup_vec, 5)
            dve.reciprocal(lam[:, 2:3], lam[:, 1:2]).then_inc(setup_vec, 1)
            dve.wait_ge(setup_vec, 6)
            dve.tensor_scalar(lam[:, 3:4], lam[:, 2:3], 0.01, 0.99, ALU.mult, ALU.add).then_inc(setup_vec, 1)

            def projection_weights():
                dve.wait_ge(params_loaded, 16)
                dve.reduce_sum(out_stat[:, 0:1], P("attn_out"), axis=AX_X).then_inc(w_out_step, 1)
                dve.tensor_scalar(pool_w128[:], ones[:, 0:128], P("pool_w"), None, ALU.mult).then_inc(w_out_step, 1)
                dve.wait_ge(w_out_step, 2)
                dve.tensor_scalar(out_stat[:, 1:2], out_stat[:, 0:1], 1.0 / D, None, ALU.mult)\
                    .then_inc(w_out_step, 1)
                dve.wait_ge(w_out_step, 3)
                dve.tensor_scalar(w_out_c[:], P("attn_out"), out_stat[:, 1:2], None, ALU.subtract)\
                    .then_inc(w_out_step, 1)

            def projection_bias():
                dve.wait_ge(v_done, 1)
                dve.tensor_tensor(out_stat[:, 3:4], P("b_attn_out"), bank(VALUE, 1, at=2 * D), ALU.subtract)\
                    .then_inc(w_out_step, 1)

            def decay_tables():
                dve.wait_ge(decay_ready, 2)
                dve.tensor_scalar(decay_q[:], decay_q[:], float(HEAD) ** -0.5, None, ALU.mult)\
                    .then_inc(decay_ready, 1)
                dve.wait_ge(decay_ready, 3)
                dve.tensor_tensor(decay_heads[:], decay_q[:, 0:PATCHES].unsqueeze(1).to_broadcast([128, HEADS, PATCHES]),
                                  P("head_mask").unsqueeze(2).to_broadcast([128, HEADS, PATCHES]), ALU.mult)\
                    .then_inc(decay_ready, 1)

            def add_positions(a):
                dve.wait_ge(early_params_loaded, 16)
                dve.wait_ge(embed_done, a + 1)
                dve.scalar_tensor_tensor(out=shaped(x_tok[:, a, :]), in0=shaped(tok_bank(a, 0)), scalar=P("b_patch"),
                                         in1=P("pos").unsqueeze(1).to_broadcast([128, BATCH // 2, PATCHES]),
                                         op0=ALU.add, op1=ALU.add).then_inc(x_ready, 1)

            def coordinates(a):
                dve.wait_ge(coords_done, a + 1)
                dve.tensor_scalar(coord_spin[0:COORDS, a, :], bank(2 * a + 1, TOK_HALF, slice(0, COORDS)),
                                  P("b_coord_spinor")[0:COORDS, :], None, ALU.add).then_inc(coords_ready, 1)

            def enhance(a):
                dve.wait_ge(manifold_ready, a + 1)
                dve.tensor_tensor(manifold[:, a, :], manifold[:, a, :], tok_bank(a, 1), ALU.mult)\
                    .then_inc(enh_mul, 1)
                dve.wait_ge(enh_mul, a + 1)
                dve.tensor_tensor(x_enh[:, a, :], manifold[:, a, :], x_tok[:, a, :], ALU.add)\
                    .then_inc(enh_ready, 1)

            def tok_normalize(a):
                dve.wait_ge(tok_rstd_ready, a + 1)
                dve.scalar_tensor_tensor(out=tok_n[:, a, :], in0=tok_bank(a, 0), scalar=P("tok_gamma"),
                                         in1=tok_rstd[:, a, :], op0=ALU.mult, op1=ALU.mult).then_inc(tok_mul, 1)
                dve.wait_ge(tok_mul, a + 1)
                dve.tensor_scalar(tok_n[:, a, :], tok_n[:, a, :], P("tok_beta"), None, ALU.add)\
                    .then_inc(tok_normed, 1)

            def tokens_out(a):
                dve.wait_ge(tok_out_done, a + 1)
                dve.tensor_scalar(set_view(h, IMG_A + a), shaped(tok_bank(a, 0)), P("b_tok_out"), None,
                                  ALU.add).then_inc(tok_in_h, 1)

            def normalize_set(s):
                dve.wait_ge(ln1_rstd_ready[s], 1)
                dve.tensor_tensor(set_view(xn, s), shaped(set_bank(s, 0)), shaped(dense(rstd1, s)),
                                  ALU.mult).then_inc(ln1_normed[s], 1)

            def elu_q(s):
                dve.wait_ge(q_parts_ready[s], 2)
                dve.scalar_tensor_tensor(out=dense(q_pos, s), in0=dense(q_exp, s), scalar=1.0, in1=dense(q_pos, s),
                                         op0=ALU.min, op1=ALU.add).then_inc(q_elu_ready[s], 1)

            def spread_heads(s, n):
                heads = slice(4 * n, 4 * n + 4)
                by_batch = q_heads[:, heads, :].rearrange("p h (b l) -> p h b l", b=BATCH)
                half = slice((s - IMG_A) * BATCH // 2, (s - IMG_A + 1) * BATCH // 2)
                dve.wait_ge(q_elu_ready[s], 1)
                for b in range(half.start, half.stop):
                    at = (b - half.start) * PATCHES
                    dve.tensor_tensor(by_batch[:, :, b, 0:PATCHES],
                                      dense(q_pos, s)[:, at:at + PATCHES].unsqueeze(1).to_broadcast([128, 4, PATCHES]),
                                      decay_heads[:, heads, :], ALU.mult).then_inc(q_heads_spread[s - IMG_A], 1)

            def elu_k(s):
                if s in (TEXT_B, IMG_B):
                    dve.wait_ge(k_parts_ready[s], 2)
                else:
                    dve.wait_ge(k_parts_ready[s], 1)
                    dve.tensor_scalar(dense(k_pos, s), set_bank(s, 3), P("b_k"), 0.0, ALU.add, ALU.max)\
                        .then_inc(k_pos_ready[s], 1)
                    dve.wait_ge(k_pos_ready[s], 1)
                dve.scalar_tensor_tensor(out=dense(k_pos, s), in0=dense(k_exp, s), scalar=1.0, in1=dense(k_pos, s),
                                         op0=ALU.min, op1=ALU.add).then_inc(k_elu_ready[s], 1)

            def decay_queries(s):
                dve.wait_ge(q_elu_ready[s], 1)
                dve.tensor_tensor(set_view(q_dec, s), shaped(dense(q_pos, s)), set_decay(decay_q, s),
                                  ALU.mult).then_inc(q_dec_ready[s], 1)

            def decay_keys(s):
                dve.wait_ge(k_elu_ready[s], 1)
                dve.tensor_tensor(set_view(k_dec, s), shaped(dense(k_pos, s)), set_decay(decay_k, s),
                                  ALU.mult).then_inc(k_dec_ready[s], 1)

            def running_sums(a):
                dve.wait_ge(k_dec_ready[TEXT_A + a], 1)
                dve.wait_ge(k_dec_ready[IMG_A + a], 1)
                for b in range(a * BATCH // 2, (a + 1) * BATCH // 2):
                    dve.tensor_tensor_scan(bcols(k_sum, b), ones[:], bcols(k_dec, b), 0.0,
                                           ALU.mult, ALU.add).then_inc(k_sum_ready, 1)

            def add_beta(a):
                half = slice(a * COLS // 2, (a + 1) * COLS // 2)
                dve.wait_ge(text_loaded[a], 16)
                dve.wait_ge(tok_in_h, a + 1)
                dve.tensor_scalar(h_beta[:, half], h[:, half], P("attn_beta"), None, ALU.add)\
                    .then_inc(h_beta_ready, 1)

            add_positions(0)
            coordinates(0)
            enhance(0)
            add_positions(1)
            normalize_set(TEXT_A)
            coordinates(1)
            tok_normalize(0)
            enhance(1)
            tokens_out(0)
            decay_tables()
            elu_q(TEXT_A)
            decay_queries(TEXT_A)
            tok_normalize(1)
            normalize_set(IMG_A)
            elu_k(TEXT_A)
            tokens_out(1)
            elu_q(IMG_A)
            elu_k(IMG_A)
            spread_heads(IMG_A, 0)
            normalize_set(TEXT_B)
            normalize_set(IMG_B)
            spread_heads(IMG_A, 1)
            projection_weights()
            running_sums(0)

            def add_value_bias(b):
                dve.wait_ge(v_done, b + 1)
                if b >= 2:
                    dve.wait_ge(av_done, b - 1)
                for rows, at, dst, first in ((slice(0, 128), 0, v_lo[b % 2], 0), (hi_rows(0), D, v_hi[b % 2], 0),
                                             (hi_rows(1), D, v_hi[b % 2], D // 2)):
                    n = dst.shape[1] * HEAD
                    halves = dst[rows, :, :].rearrange("p (j r) (a c) -> p j (r a) c", r=2, a=2)[:, :, 0:4:3, :]
                    dve.tensor_tensor(halves, bank(VALUE, n, rows, at).rearrange("p (j r c) -> p j r c", r=2, c=HEAD),
                                      P("bias_v")[rows, first:first + n].rearrange("p (j r c) -> p j r c", r=2, c=HEAD),
                                      ALU.add).then_inc(v_ready, 1)

            def mask_lo(b, n):
                dve.wait_ge(lo_done, 2 * b + n + 1)
                dve.tensor_tensor(s_lo[b % 2][:, 4 * n:4 * n + 4, 0:LO],
                                  bank(LO_A + n, 4 * LO).rearrange("p (a l) -> p a l", a=4),
                                  P("causal").unsqueeze(1).to_broadcast([128, 4, LO]),
                                  ALU.mult).then_inc(lo_masked, 1)

            def mask_high(b):
                dve.wait_ge(high_done, b + 1)
                for n in range(2):
                    rows = hi_rows(n)
                    dve.tensor_tensor(s_hi[b % 2][rows], bank(HIGH, 4 * HI, rows).rearrange("p (a l) -> p a l", a=4),
                                      P("causal_hi")[rows].unsqueeze(1).to_broadcast([HI, 4, HI]),
                                      ALU.mult).then_inc(high_masked, 1)

            def divide(b):
                dve.wait_ge(rden_ready, b // PER + 1)
                dve.wait_ge(av_done, b + 1)
                dve.tensor_tensor(bcols(att, b), bank(AV, SEQ), bcols(rden, b), ALU.mult).then_inc(att_ready, 1)

            def residual(g):
                dve.wait_ge(out_rstd_ready, g + 1)
                if g >= 2:
                    dve.wait_ge(h1_ready, g - 1)
                dve.scalar_tensor_tensor(out=attn_x[:, g % 2, :], in0=bank(post_x(g)), scalar=out_stat[:, 3:4],
                                         in1=rstd2[:, g % 2, :], op0=ALU.add, op1=ALU.mult).then_inc(out_mul, 1)
                dve.wait_ge(h_beta_ready, g // 2 + 1)
                dve.wait_ge(out_mul, g + 1)
                dve.scalar_tensor_tensor(out=gcols(h1, g), in0=attn_x[:, g % 2, :], scalar=P("attn_gamma"),
                                         in1=gcols(h_beta, g), op0=ALU.mult, op1=ALU.add).then_inc(h1_ready, 1)

            def normalize_h1(g):
                dve.wait_ge(h1_rstd_ready, g + 1)
                dve.tensor_tensor(gcols(xn3, g), bank(post_x(g)), rstd2[:, g % 2, :], ALU.mult).then_inc(h1_normed, 1)

            def score_shifts(g):
                two = slice(PER * g, PER * g + PER)
                dve.wait_ge(score_done, g + 1)
                dve.tensor_reduce(score_neg_max[:, two], bank(post_x(g)).rearrange("p (b l) -> p b l", b=PER),
                                  axis=AX_X, op=ALU.max, negate=True).then_inc(score_max_ready, 1)
                dve.wait_ge(score_max_ready, g + 1)
                dve.tensor_scalar(score_bias[:, two], score_neg_max[:, two], P("pool_b"), P("pool_b"), ALU.subtract,
                                  ALU.add).then_inc(score_bias_ready, 1)

            def pool_group(g):
                two = slice(PER * g, PER * g + PER)
                for b in (PER * g, PER * g + 1):
                    dve.wait_ge(pool_exp_ready, b + 1)
                    dve.scalar_tensor_tensor(out=bcols(pool_prod, b), in0=bcols(xn3, b), scalar=1.0,
                                             in1=bcols(pool_exp, b), op0=ALU.mult, op1=ALU.mult,
                                             accum_out=pooled_raw[:, b:b + 1]).then_inc(pooled_step, 1)
                dve.reciprocal(exp_rsum[:, two], exp_sum[:, two]).then_inc(pooled_step, 1)
                dve.wait_ge(pooled_step, 3 * (g + 1))
                dve.tensor_tensor(pooled[:, two], pooled_raw[:, two], exp_rsum[:, two], ALU.mult)\
                    .then_inc(pooled_ready, 1)

            def gate_logits(g):
                dve.wait_ge(gate_done, g + 1)
                dve.tensor_tensor(gl[:, g, 0, :], bank(POST_Y, EXPERTS, slice(0, PER)), P("bias_gate")[0:PER, :],
                                  ALU.add).then_inc(gate_logits_ready, 1)
                dve.wait_ge(gate_logits_ready, g + 1)
                dve.tensor_reduce(gl[:, g, 1, 0:1], gl[:, g, 0, :], axis=AX_X, op=ALU.max, negate=True)\
                    .then_inc(gate_shift_ready, 1)

            def gate_top(g):
                n = 8 * g
                row = gl[:, g, 1, :]
                dve.wait_ge(gate_exp_ready, g + 1)
                dve.reciprocal(row[:, 2:3], row[:, 1:2]).then_inc(gate_step, 1)
                dve.wait_ge(gate_step, n + 1)
                dve.tensor_scalar(gl[:, g, 3, :], gl[:, g, 2, :], row[:, 2:3], None, ALU.mult).then_inc(gate_step, 1)
                dve.wait_ge(gate_step, n + 2)
                dve.max(gl[:, g, 4, :], gl[:, g, 3, :]).then_inc(gate_step, 1)
                dve.wait_ge(gate_step, n + 3)
                dve.max_index(gate_idx[:, g, :], gl[:, g, 4, :], gl[:, g, 3, :]).then_inc(gate_step, 1)
                dve.scalar_tensor_tensor(out=row[:, 3:4], in0=gl[:, g, 4, 0:1], scalar=1e-9, in1=gl[:, g, 4, 1:2],
                                         op0=ALU.add, op1=ALU.add).then_inc(gate_step, 1)
                dve.wait_ge(gate_step, n + 5)
                dve.tensor_copy(gate_cat[:, g, 1, :], gate_idx[:, g, 0:TOP]).then_inc(gate_step, 1)
                dve.reciprocal(row[:, 4:5], row[:, 3:4]).then_inc(gate_step, 1)
                dve.wait_ge(gate_step, n + 7)
                dve.tensor_scalar(gate_cat[:, g, 0, :], gl[:, g, 4, 0:TOP], row[:, 4:5], None, ALU.mult)\
                    .then_inc(gate_step, 1)
                dve.wait_ge(gate_step, n + 8)
                for kind in range(2):
                    dve.tensor_tensor(gate_rows[:, g, kind, :].rearrange("p (b s) -> p b s", s=TOP),
                                      P("diag")[0:PER, 0:PER * TOP].rearrange("p (b s) -> p b s", s=TOP),
                                      gate_cat[:, g, kind, :].unsqueeze(1).to_broadcast([PER, PER, TOP]),
                                      ALU.mult).then_inc(gate_rows_ready, 1)

            def shift_gates(g):
                dve.wait_ge(gate_shift_ready, g + 1)
                dve.tensor_scalar(gl[:, g, 4, :], gl[:, g, 0, :], gl[:, g, 1, 0:1], None, ALU.add)\
                    .then_inc(gates_shifted, 1)

            def sum_gates(g):
                dve.wait_ge(gate_exp_ready, g + 1)
                dve.reduce_sum(gl[:, g, 1, 1:2], gl[:, g, 2, :], axis=AX_X).then_inc(gates_summed, 1)
                dve.wait_ge(gates_summed, g - LATE_GROUPS[0] + 1)

            def keep_gates(g):
                n = PER * TOP
                dve.wait_ge(gate_bcast_done, g + 1)
                dve.tensor_copy(gate_all[:, g * n:(g + 1) * n], bank(POST_X if g == GROUPS - 1 else POST_Y, n)).then_inc(gates_ready, 1)
                dve.tensor_copy(expert_of[:, g * n:(g + 1) * n], bank(POST_X if g == GROUPS - 1 else POST_Y, n, slice(0, 1), at=n))\
                    .then_inc(gates_ready, 1)

            dve.wait_ge(v_zeroed, 5)
            for b in range(BATCH):
                g = b // 2
                if b == 0:
                    projection_bias()
                add_value_bias(b)
                if b % 2 == 0:
                    mask_lo(b, 0)
                    if g >= 2:
                        normalize_h1(g - 2)
                    mask_lo(b, 1)
                    mask_high(b)
                    if g >= 2:
                        score_shifts(g - 2)
                    if b >= 1:
                        divide(b - 1)
                    if g >= 3:
                        gate_top(g - 3)
                else:
                    if g >= 2:
                        pool_group(g - 2)
                    mask_lo(b, 0)
                    if g >= 3:
                        keep_gates(g - 3)
                    mask_lo(b, 1)
                    if g >= 1 and b < BATCH - 1:
                        residual(g - 1)
                    mask_high(b)
                    if g >= 2:
                        gate_logits(g - 2)
                    divide(b - 1)
                    if b == BATCH - 1:
                        residual(g - 1)
                if b == 0:
                    elu_q(TEXT_B)
                    elu_k(TEXT_B)
                    elu_q(IMG_B)
                    elu_k(IMG_B)
                elif b == 1:
                    decay_keys(IMG_B)
                    running_sums(1)
                elif b == 2:
                    spread_heads(IMG_B, 0)
                    add_beta(0)
                elif b == 3:
                    spread_heads(IMG_B, 1)
                elif b == 4:
                    add_beta(1)
            last = GROUPS - 1

            def fetch(u, k):
                if not isinstance(u, int) or u >= 4:
                    dve.wait_ge(eo_ready, u - 3)
                e = dve.value_load(expert_of[0:1, bass.ds(u, 1)], min_val=0, max_val=EXPERTS - 1)
                dve.tensor_copy(w_fix[k], expert_w[:, bass.ds(e, 1), :].rearrange("p a n -> p (a n)"))\
                    .then_inc(w_fixed, 1)

            def combine(b, u):
                dve.wait_ge(eo_ready, u + 1)
                dve.scalar_tensor_tensor(out=acc, in0=eo[0], scalar=gate_all[:, bass.ds(u, 1)],
                                         in1=rcols(h1, b), op0=ALU.mult, op1=ALU.add).then_inc(acc_ready, 1)

            def combine_last(b, u):
                dve.wait_ge(acc_ready, u)
                dve.wait_ge(eo_ready, u + 1)
                dve.scalar_tensor_tensor(out=rcols(out_sb, b), in0=eo[1], scalar=gate_all[:, bass.ds(u, 1)],
                                         in1=acc, op0=ALU.mult, op1=ALU.add).then_inc(acc_ready, 1)
                dve.wait_ge(acc_ready, u + 1)

            dve.wait_ge(experts_loaded, 16)
            dve.wait_ge(high_done, BATCH)
            divide(BATCH - 1)
            fetch(0, 0)
            normalize_h1(last - 1)
            fetch(1, 1)
            residual(last)
            gate_top(last - 2)
            score_shifts(last - 1)
            fetch(2, 2)
            keep_gates(last - 2)
            fetch(3, 3)
            normalize_h1(last)
            score_shifts(last)
            pool_group(last - 1)
            pool_group(last)
            gate_logits(last - 1)
            shift_gates(last - 1)
            gate_logits(last)
            shift_gates(last)
            combine(0, 0)
            fetch(4, 0)
            sum_gates(last - 1)
            gate_top(last - 1)
            combine_last(0, 1)
            fetch(5, 1)
            sum_gates(last)
            gate_top(last)
            combine(1, 2)
            fetch(6, 2)
            combine_last(1, 3)
            fetch(7, 3)
            keep_gates(last - 1)
            keep_gates(last)
            dve.wait_ge(gates_ready, 2 * GROUPS)
            with dve.Fori(1, UNITS // 4 - 1) as i:
                for n in range(2):
                    u = i * 4 + 2 * n
                    combine(i * 2 + n, u)
                    fetch(u + 4, 2 * n)
                    combine_last(i * 2 + n, u + 1)
                    fetch(u + 5, 2 * n + 1)

            for n in range(2):
                combine(BATCH - 2 + n, UNITS - 4 + 2 * n)
                combine_last(BATCH - 2 + n, UNITS - 3 + 2 * n)

        @block.tensor
        def _(pe):
            def mm(*args, **kw):
                return nc.tensor.matmul(*args, **kw)

            qkv = P("qkv")
            center = P("center")
            mean = P("ones_mean")

            def keep_warm(products, at):
                for _ in range(products):
                    mm(bank(at, SEQ), ones[:, 0:128], ones[:], start=True, stop=True)

            def embed(a, first, end):
                pe.wait_ge(patches_loaded[a], 16)
                for c in range(first, end):
                    last = mm(tok_bank(a, 0), patch_w[:, c, :], patch_in[:, a, c, :], start=(c == 0),
                              stop=(c == PATCH_CHUNKS - 1))
                if end == PATCH_CHUNKS:
                    last.then_inc(embed_done, 1)

            def coordinates(a):
                pe.wait_ge(x_ready, a + 1)
                mm(tok_bank(a, 1), P("coord_spinor"), x_tok[:, a, :], start=True, stop=True)\
                    .then_inc(coords_done, 1)

            def manifolds(a):
                pe.wait_ge(coords_ready, a + 1)
                pe.wait_ge(spinor_ready, a + 1)
                mm(tok_bank(a, 0), P("embed"), coord_spin[:, a, :], start=True, stop=True)
                mm(tok_bank(a, 1), P("spinor_sum"), coord_spin[:, a, :], start=True, stop=True)\
                    .then_inc(manifold_done, 1)

            def tok_center(a):
                pe.wait_ge(enh_ready, a + 1)
                mm(tok_bank(a, 0), center, x_enh[:, a, :], start=True, stop=True).then_inc(tok_centered, 1)

            def tok_variance(a):
                pe.wait_ge(tok_squared, a + 1)
                mm(tok_bank(a, 1), mean, tok_sq[:, a, :], start=True, stop=True).then_inc(tok_var_done, 1)

            def tok_project(a):
                pe.wait_ge(tok_normed, a + 1)
                mm(tok_bank(a, 0), P("tok_out"), tok_n[:, a, :], start=True, stop=True).then_inc(tok_out_done, 1)

            def center_set(s):
                if s >= IMG_A:
                    pe.wait_ge(tok_in_h, s - IMG_A + 1)
                else:
                    pe.wait_ge(text_loaded[s], 16)
                mm(set_bank(s, 0), center, set_view(h, s), start=True, stop=True).then_inc(ln1_centered[s], 1)

            def variance_set(s):
                pe.wait_ge(ln1_squared[s], 1)
                mm(set_bank(s, 1), mean, dense(sq1, s), start=True, stop=True).then_inc(ln1_var_done[s], 1)

            def project_q(s):
                pe.wait_ge(ln1_normed[s], 1)
                mm(set_bank(s, 2), qkv[:, 0:D], set_view(xn, s), start=True, stop=True).then_inc(q_done[s], 1)

            def project_k(s):
                pe.wait_ge(ln1_normed[s], 1)
                mm(set_bank(s, 3), qkv[:, D:2 * D], set_view(xn, s), start=True, stop=True).then_inc(k_done[s], 1)

            pe.wait_ge(setup_vec, 3)
            keep_warm(WARM_UPS, POST_Y)
            pe.wait_ge(patch_w_loaded, 16)
            embed(0, 0, PATCH_CHUNKS)
            pe.wait_ge(early_params_loaded, 16)
            center_set(TEXT_A)
            coordinates(0)
            embed(1, 0, PATCH_CHUNKS // 2)
            manifolds(0)
            variance_set(TEXT_A)
            embed(1, PATCH_CHUNKS // 2, PATCH_CHUNKS)
            tok_center(0)
            coordinates(1)
            tok_variance(0)
            manifolds(1)
            pe.wait_ge(params_loaded, 16)
            project_q(TEXT_A)
            tok_project(0)
            project_k(TEXT_A)
            tok_center(1)
            center_set(IMG_A)
            tok_variance(1)
            variance_set(IMG_A)
            center_set(TEXT_B)
            tok_project(1)
            project_q(IMG_A)
            project_k(IMG_A)
            variance_set(TEXT_B)
            center_set(IMG_B)
            variance_set(IMG_B)

            def denominators(g):
                pe.wait_ge(qk_sum_ready, g + 1)
                if g >= 2:
                    pe.wait_ge(den_log_ready, g - 1)
                elif g == 0:
                    pe.wait_ge(k_parts_ready[TEXT_B], 2)
                mm(bank(POST_X + g % 2), P("block_ones"), gcols(qk_sum, g), start=True, stop=True)\
                    .then_inc(den_done, 1)

            def values(b):
                if b == 0:
                    pe.wait_ge(k_pos_ready[TEXT_A], 1)
                else:
                    pe.wait_ge(v_ready, 3 * b)
                if b == 1:
                    pe.wait_ge(w_out_step, 5)
                at = b * SEQ
                mm(bank(VALUE, D), xn[:, at:at + LO], qkv[:, 2 * D:3 * D], start=True, stop=True)
                if b == 0:
                    mm(bank(VALUE, 1, at=2 * D), mean, P("b_attn_out"), start=True, stop=True)
                for n in range(2):
                    last = mm(bank(VALUE, D // 2, hi_rows(n), at=D), xn[:, at + LO:at + SEQ],
                              qkv[:, 2 * D + n * D // 2:2 * D + (n + 1) * D // 2], start=True, stop=True)
                last.then_inc(v_done, 1)

            def scores_lo(b, n):
                at = b * SEQ
                if b % 4 == 0:
                    pe.wait_ge(q_heads_loaded[b // 4 * 2 + n], 16 * HEADS // 2)
                pe.wait_ge(q_heads_spread[b // 4], 4 * n + 4)
                pe.wait_ge(k_dec_ready[TEXT_A + b // 4], 1)
                pe.wait_ge(k_dec_ready[IMG_A + b // 4], 1)
                if b >= 1:
                    pe.wait_ge(lo_masked, 2 * b - 1 + n)
                mm(bank(LO_A + n, 4 * LO), k_dec[:, at:at + LO], q_heads[:, 4 * n:4 * n + 4, at:at + LO],
                   start=True, stop=True).then_inc(lo_done, 1)

            def scores_tail(b):
                at = b * SEQ
                if b == 0:
                    pe.wait_ge(q_parts_ready[IMG_B], 2)
                else:
                    pe.wait_ge(tail_copied, b)
                mm(bank(TAIL, HEADS * HI), k_dec[:, at:at + LO], q_heads[:, :, at + LO:at + SEQ],
                   start=True, stop=True).then_inc(tail_done, 1)

            def scores_high(b):
                at = b * SEQ
                if b == 0:
                    pe.wait_ge(k_parts_ready[IMG_B], 2)
                else:
                    pe.wait_ge(high_masked, 2 * b)
                for n in range(2):
                    last = mm(bank(HIGH, 4 * HI, hi_rows(n)), k_dec[:, at + LO:at + SEQ],
                              q_heads[:, 4 * n:4 * n + 4, at + LO:at + SEQ], start=True, stop=True)
                last.then_inc(high_done, 1)

            def attend(b):
                pe.wait_ge(v_ready, 3 * b + 3)
                pe.wait_ge(lo_masked, 2 * b + 2)
                pe.wait_ge(tail_copied, b + 1)
                pe.wait_ge(high_masked, 2 * b + 2)
                if b >= 1:
                    pe.wait_ge(att_ready, b)
                p = b % 2
                for r in range(2):
                    for j in range(HEADS // 2):
                        mm(bank(AV, SEQ, slice(32 * j, 32 * j + 32)), v_lo[p][:, 2 * j + r, :],
                           s_lo[p][:, 2 * j + r, :], start=(r == 0), stop=False)
                    for j in range(HEADS // 2):
                        rows, at_head = hi_rows(j // 2), 2 * (j % 2) + r
                        last = mm(bank(AV, HI, slice(32 * j, 32 * j + 32), at=LO), v_hi[p][rows, at_head, :],
                                  s_hi[p][rows, at_head, :], start=False, stop=(r == 1))
                last.then_inc(av_done, 1)

            def project_out(g):
                pe.wait_ge(att_ready, PER * (g + 1))
                if g == 0:
                    pe.wait_ge(den_log_ready, 3)
                elif g < GROUPS - 1:
                    pe.wait_ge(pool_exp_ready, PER * g)
                mm(bank(post_x(g)), w_out_c[:], gcols(att, g), start=True, stop=True).then_inc(out_done, 1)

            def variance_out(g):
                pe.wait_ge(out_squared, g + 1)
                if g == 0:
                    pe.wait_ge(den_log_ready, 4)
                elif g == 2:
                    pe.wait_ge(gates_ready, 2 * (g - 1))
                mm(bank(post_y(g)), mean, sq2[:, g % 2, :], start=True, stop=True).then_inc(out_var_done, 1)

            def center_h1(g):
                pe.wait_ge(h1_ready, g + 1)
                mm(bank(post_x(g)), center, gcols(h1, g), start=True, stop=True).then_inc(h1_centered, 1)

            def variance_h1(g):
                pe.wait_ge(h1_squared, g + 1)
                if 1 <= g < GROUPS - 1:
                    pe.wait_ge(gate_logits_ready, g)
                mm(bank(post_y(g)), mean, sq2[:, g % 2, :], start=True, stop=True).then_inc(h1_var_done, 1)

            def pool_scores(g):
                pe.wait_ge(h1_normed, g + 1)
                mm(bank(post_x(g)), pool_w128[:], gcols(xn3, g), start=True, stop=True).then_inc(score_done, 1)

            def gates(g):
                pe.wait_ge(pooled_ready, g + 1)
                if g < GROUPS - 2:
                    pe.wait_ge(out_log, g + 2)
                elif g == GROUPS - 2:
                    pe.wait_ge(gates_ready, 2 * g)
                else:
                    pe.wait_ge(gate_logits_ready, g)
                mm(bank(POST_Y, EXPERTS, slice(0, PER)), pooled[:, PER * g:PER * g + PER], P("gate"),
                   start=True, stop=True).then_inc(gate_done, 1)

            def spread_gates(g):
                pe.wait_ge(gate_rows_ready, 2 * (g + 1))
                if g < GROUPS - 2:
                    pe.wait_ge(h1_log, g + 2)
                elif g == GROUPS - 2:
                    pe.wait_ge(gate_logits_ready, GROUPS)
                else:
                    pe.wait_ge(pool_exp_ready, BATCH - PER)
                mm(bank(POST_X if g == GROUPS - 1 else POST_Y, 2 * PER * TOP), ones[0:PER, 0:128], gate_rows[:, g, :, :].rearrange("p k n -> p (k n)"),
                   start=True, stop=True).then_inc(gate_bcast_done, 1)

            for b in range(BATCH):
                g = b // 2
                values(b)
                if b % 2 == 0 and g >= 2:
                    center_h1(g - 2)
                scores_lo(b, 0)
                if b % 2 == 1 and g >= 3:
                    spread_gates(g - 3)
                if b % 2 == 1 and g >= 1:
                    project_out(g - 1)
                if b % 2 == 0 and g >= 2:
                    variance_h1(g - 2)
                if b == 0:
                    project_q(TEXT_B)
                    project_q(IMG_B)
                    project_k(IMG_B)
                    project_k(TEXT_B)
                scores_lo(b, 1)
                if b % 2 == 1 and g >= 1:
                    variance_out(g - 1)
                scores_tail(b)
                scores_high(b)
                if b % 2 == 0 and g >= 2:
                    pool_scores(g - 2)
                if b % 2 == 1 and g >= 2:
                    gates(g - 2)
                if b < 2:
                    denominators(b)
                elif b == 2:
                    denominators(2)
                    denominators(3)
                if b >= 1:
                    attend(b - 1)
            last = GROUPS - 1

            def up(u, k, b):
                pe.wait_ge(w_fixed, u + 1)
                if not isinstance(u, int) or u >= 2:
                    pe.wait_ge(hid_ready, u * 4 - 4)
                for c in range(HID_CHUNKS):
                    last = mm(bank(2 * (k % 2) + c // 2, SEQ, at=(c % 2) * SEQ),
                              w_fix[k][:, W1_AT + 128 * c:W1_AT + 128 * (c + 1)], rcols(xn3, b), start=True, stop=True)
                    if c % 2:
                        last.then_inc(up_done, 1)

            def down(u, k):
                pe.wait_ge(hid_ready, u * 4 + 4)
                if not isinstance(u, int) or u >= 2:
                    pe.wait_ge(eo_ready, u - 1)
                for c in range(HID_CHUNKS):
                    last = mm(bank(4 + k % 2, SEQ), w_fix[k][:, W2_AT + 128 * c:W2_AT + 128 * (c + 1)],
                              hid[k % 2][:, c, :], start=(c == 0), stop=(c == HID_CHUNKS - 1))
                last.then_inc(down_done, 1)

            attend(BATCH - 1)
            center_h1(last - 1)
            project_out(last)
            variance_h1(last - 1)
            variance_out(last)
            up(0, 0, 0)
            pool_scores(last - 1)
            up(1, 1, 0)
            center_h1(last)
            spread_gates(last - 2)
            variance_h1(last)
            up(2, 2, 1)
            pool_scores(last)
            pe.wait_ge(pool_exp_ready, BATCH - PER)
            keep_warm(5, POST_X)
            gates(last - 1)
            pe.wait_ge(pool_exp_ready, BATCH)
            pe.wait_ge(h1_log, GROUPS)
            down(0, 0)
            gates(last)
            keep_warm(3, POST_X)
            down(1, 1)
            up(3, 3, 1)
            down(2, 2)
            for k in range(4):
                up(4 + k, k, 2 + k // TOP)
                down(3 + k, (k + 3) % 4)
                if k in (0, 1):
                    spread_gates(LATE_GROUPS[k])
            with pe.Fori(2, UNITS // 4) as i:
                for k in range(4):
                    up(i * 4 + k, k, i * 2 + k // 2)
                    down(i * 4 + (k - 1), (k + 3) % 4)
            down(UNITS - 1, 3)


def _param_array(t):
    prm = np.zeros((128, PARAM_COLS), np.float32)

    def put(name, a, row=0):
        at, n = AT[name]
        a = np.asarray(a, np.float32)
        a = a[:, None] if a.ndim == 1 else a
        prm[row:row + a.shape[0], at:at + a.shape[1]] = a

    at, _ = AT["coord_spinor"]
    put("coord_spinor", t["L0_tok_W_coord"])
    prm[:, at + SPINOR_AT:at + SPINOR_AT + SPINOR] = t["L0_tok_W_spinor"]
    put("embed", t["L0_tok_W_embed"])
    put("tok_out", t["L0_tok_W_out"])
    put("qkv", t["L0_attn_W_qkv"])
    put("attn_out", t["L0_attn_W_out"])
    put("gate", t["L0_ffn_gate_w"])
    put("bias_v", np.broadcast_to(t["L0_attn_b_qkv"][2 * D:], (128, D)))
    put("bias_gate", np.broadcast_to(t["L0_ffn_gate_b"], (128, EXPERTS)))
    put("pos", t["L0_tok_pos_embed"][0].T)
    put("ones_mean", np.full((128, D), 1.0 / D))
    put("center", np.eye(D) - 1.0 / D)
    put("spinor_sum", np.ones((SPINOR, D)), SPINOR_AT)
    head_of = np.arange(D) // HEAD
    put("block_ones", head_of[:, None] == head_of[None, :])
    put("causal", np.arange(LO)[None, :] >= np.arange(128)[:, None])
    for n in range(2):
        put("causal_hi", np.arange(HI)[None, :] >= np.arange(HI)[:, None], 64 * n)
    put("position", np.broadcast_to(np.arange(SEQ), (128, SEQ)))
    put("head_mask", head_of[:, None] == np.arange(HEADS)[None, :])
    put("diag", np.repeat(np.eye(BATCH), TOP, axis=1))
    put("b_patch", t["L0_tok_b_patch"])
    put("b_coord_spinor", t["L0_tok_b_coord"])
    put("b_coord_spinor", t["L0_tok_b_spinor"], SPINOR_AT)
    put("b_embed", t["L0_tok_b_embed"])
    put("tok_gamma", t["L0_tok_ln_gamma"])
    put("tok_beta", t["L0_tok_ln_beta"])
    put("b_tok_out", t["L0_tok_b_out"])
    put("b_q", t["L0_attn_b_qkv"][:D])
    put("b_k", t["L0_attn_b_qkv"][D:2 * D])
    put("b_attn_out", t["L0_attn_b_out"])
    put("decay", np.repeat(t["L0_attn_decay_logits"], HEAD))
    put("attn_gamma", t["L0_attn_ln_g"])
    put("attn_beta", t["L0_attn_ln_b"])
    put("pool_w", t["L0_ffn_attn_w"])
    put("pool_b", np.broadcast_to(t["L0_ffn_attn_b"], (128,)))
    return prm


def kernel(**inputs):
    import concourse.bacc as _bacc
    from concourse.bass_utils import run_bass_kernel_spmd as _run

    t = {k: np.asarray(v) for k, v in inputs.items()}
    patches = t["x"].reshape(BATCH, CHANNELS, GRID, PATCH, GRID, PATCH).transpose(1, 3, 5, 0, 2, 4)
    arrays = {
        "patches": patches.reshape(PATCH_CHUNKS, 128, 2, TOK_HALF).transpose(1, 2, 0, 3),
        "text": t["txt"].transpose(2, 0, 1),
        "w_patch": t["L0_tok_W_patch"].reshape(PATCH_CHUNKS, 128, D).transpose(1, 0, 2),
        "params": _param_array(t),
        "experts": np.concatenate([
            t["L0_ffn_w1"].transpose(1, 0, 2),
            t["L0_ffn_w2"].reshape(EXPERTS, HID_CHUNKS, 128, D).transpose(2, 0, 1, 3).reshape(128, EXPERTS, HIDDEN),
            t["L0_ffn_b1"].reshape(EXPERTS, HID_CHUNKS, 128).transpose(2, 0, 1),
            t["L0_ffn_b2"].T[:, :, None]], axis=2),
    }
    nc = _bacc.Bacc("TRN2", target_bir_lowering=False, num_devices=1)
    arrays = {k: np.ascontiguousarray(a) for k, a in arrays.items()}
    args = [nc.dram_tensor(k, a.shape, mybir.dt.from_np(a.dtype), kind="ExternalInput").ap()
            for k, a in arrays.items()]
    out = nc.dram_tensor("out", (D, COLS), F32, kind="ExternalOutput").ap()
    build(nc, *args, out)
    r = _run(nc, [arrays], core_ids=[0])
    return np.ascontiguousarray(r.results[0]["out"].reshape(D, BATCH, SEQ).transpose(1, 2, 0))
```
